# Optimizing a Trainium2 kernel written in Bass

```python
import numpy as np
import jax
import jax.numpy as jnp

def _softmax(x, axis=-1):
    return jax.nn.softmax(x, axis=axis)
def _gelu(x):
    return jax.nn.gelu(x, approximate=True)
def _silu(x):
    return jax.nn.silu(x)
def _sigmoid(x):
    return jax.nn.sigmoid(x)
def _layernorm(x, axis=-1, eps=1e-5):
    m = jnp.mean(x, axis=axis, keepdims=True)
    v = jnp.var(x, axis=axis, keepdims=True)
    return (x - m) / jnp.sqrt(v + eps)
def _scatter_add(tgt, idx, src, axis=0):
    return tgt.at[idx].add(src)
def _segment_sum(src, seg, n):
    return jax.ops.segment_sum(src, seg, n)

kernel_name = 'mk_dlrm_tower_d1_rec_c52f46'

def setup_inputs(seed: int = 0):
    np.random.seed(seed)
    _w = jnp.asarray
    def _rec_inputs():
        import jax
        import jax.numpy as jnp
        _tk = jax.random.key(seed)
        ids = jnp.stack([jax.random.randint(jax.random.fold_in(_tk, 200 + f), (1024,), 0, v, jnp.int32) for f, v in enumerate([1000000, 1000, 100000, 100000])], axis=1)
        tbl_0 = 0.05 * jax.random.normal(jax.random.fold_in(_tk, 500 + 0), (1000000, 4), jnp.float32)
        tbl_1 = 0.05 * jax.random.normal(jax.random.fold_in(_tk, 500 + 1), (1000, 4), jnp.float32)
        tbl_2 = 0.05 * jax.random.normal(jax.random.fold_in(_tk, 500 + 2), (100000, 4), jnp.float32)
        tbl_3 = 0.05 * jax.random.normal(jax.random.fold_in(_tk, 500 + 3), (100000, 4), jnp.float32)
        _rk = jax.random.fold_in(_tk, 7)
        r_x = 7.22013e-05 + 1.00017 * jax.random.normal(jax.random.fold_in(_rk, 101), (1024, 2048), jnp.float32)
        W_top1 = 0.0197642 * jax.random.normal(jax.random.fold_in(_tk, 801), (2560, 512), jnp.float32)
        W_top2 = 0.0441942 * jax.random.normal(jax.random.fold_in(_tk, 802), (512, 256), jnp.float32)
        W_top3 = 0.0625 * jax.random.normal(jax.random.fold_in(_tk, 803), (256, 1), jnp.float32)
        b_top1 = jnp.zeros((512,), jnp.float32)
        b_top2 = jnp.zeros((256,), jnp.float32)
        return r_x, ids, tbl_0, tbl_1, tbl_2, tbl_3, W_top1, b_top1, W_top2, b_top2, W_top3
    r_x, ids, tbl_0, tbl_1, tbl_2, tbl_3, W_top1, b_top1, W_top2, b_top2, W_top3 = _rec_inputs()
    def _L0_rec_setup():
        import jax, jax.numpy as jnp
        import numpy as np
        B, IN, HID, D, N, OUT = (4096, 2048, 2048, 512, 4, 512)
        H = 8
        HD = D // H

        def _ln(x, g, b):
            m = x.mean(-1, keepdims=True)
            v = ((x - m) ** 2).mean(-1, keepdims=True)
            return (x - m) / jnp.sqrt(v + 1e-05) * g + b
        key = jax.random.key(seed)
        ks = jax.random.split(key, 32)

        def nrm(k, shape, scale=0.02):
            return jax.random.normal(k, shape, jnp.float32) * scale
        inp = {}
        inp['x'] = jax.random.normal(ks[0], (B, IN), jnp.float32)
        inp['strength'] = jax.random.uniform(ks[1], (B, N, N), jnp.float32)
        for t, i in (('er', 2), ('ei', 4)):
            inp[t + '_W1'] = nrm(ks[i], (HID, IN))
            inp[t + '_b1'] = jnp.zeros((HID,), jnp.float32)
            inp[t + '_g1'] = jnp.ones((HID,), jnp.float32)
            inp[t + '_be1'] = jnp.zeros((HID,), jnp.float32)
            inp[t + '_W2'] = nrm(ks[i + 1], (N * D, HID))
            inp[t + '_b2'] = jnp.zeros((N * D,), jnp.float32)
        names = ['Wq_r', 'Wq_i', 'Wk_r', 'Wk_i', 'Wv_r', 'Wv_i', 'Wo_r', 'Wo_i']
        for j, nm in enumerate(names):
            inp[nm] = nrm(ks[6 + j], (D, D))
            inp['b' + nm[1:]] = jnp.zeros((D,), jnp.float32)
        inp['int_Wr'] = jnp.tile(jnp.eye(D, dtype=jnp.float32)[None], (N, 1, 1))
        inp['int_Wi'] = jnp.zeros((N, D, D), jnp.float32)
        inp['meas_Mr'] = nrm(ks[20], (OUT, D), 1.0 / np.sqrt(D))
        inp['meas_Mi'] = nrm(ks[21], (OUT, D), 1.0 / np.sqrt(D))
        inp['post_W'] = nrm(ks[22], (OUT, OUT))
        inp['post_b'] = jnp.zeros((OUT,), jnp.float32)
        inp['post_g'] = jnp.ones((OUT,), jnp.float32)
        inp['post_be'] = jnp.zeros((OUT,), jnp.float32)
        return inp
    _L0_rec_all = _L0_rec_setup()
    _L0_rec_in = {k: v for k, v in _L0_rec_all.items() if k in ('er_W1', 'er_b1', 'er_g1', 'er_be1', 'er_W2', 'er_b2', 'ei_W1', 'ei_b1', 'ei_g1', 'ei_be1', 'ei_W2', 'ei_b2', 'Wq_r', 'bq_r', 'Wq_i', 'bq_i', 'Wk_r', 'bk_r', 'Wk_i', 'bk_i', 'Wv_r', 'bv_r', 'Wv_i', 'bv_i', 'Wo_r', 'bo_r', 'Wo_i', 'bo_i', 'int_Wr', 'int_Wi', 'meas_Mr', 'meas_Mi', 'post_W', 'post_b', 'post_g', 'post_be', )}
    del _L0_rec_all

    return {
        "r_x": r_x,
        "ids": ids,
        "tbl_0": tbl_0,
        "tbl_1": tbl_1,
        "tbl_2": tbl_2,
        "tbl_3": tbl_3,
        "W_top1": W_top1,
        "b_top1": b_top1,
        "W_top2": W_top2,
        "b_top2": b_top2,
        "W_top3": W_top3,
        "L0_rec_er_W1": _L0_rec_in["er_W1"],
        "L0_rec_er_b1": _L0_rec_in["er_b1"],
        "L0_rec_er_g1": _L0_rec_in["er_g1"],
        "L0_rec_er_be1": _L0_rec_in["er_be1"],
        "L0_rec_er_W2": _L0_rec_in["er_W2"],
        "L0_rec_er_b2": _L0_rec_in["er_b2"],
        "L0_rec_ei_W1": _L0_rec_in["ei_W1"],
        "L0_rec_ei_b1": _L0_rec_in["ei_b1"],
        "L0_rec_ei_g1": _L0_rec_in["ei_g1"],
        "L0_rec_ei_be1": _L0_rec_in["ei_be1"],
        "L0_rec_ei_W2": _L0_rec_in["ei_W2"],
        "L0_rec_ei_b2": _L0_rec_in["ei_b2"],
        "L0_rec_Wq_r": _L0_rec_in["Wq_r"],
        "L0_rec_bq_r": _L0_rec_in["bq_r"],
        "L0_rec_Wq_i": _L0_rec_in["Wq_i"],
        "L0_rec_bq_i": _L0_rec_in["bq_i"],
        "L0_rec_Wk_r": _L0_rec_in["Wk_r"],
        "L0_rec_bk_r": _L0_rec_in["bk_r"],
        "L0_rec_Wk_i": _L0_rec_in["Wk_i"],
        "L0_rec_bk_i": _L0_rec_in["bk_i"],
        "L0_rec_Wv_r": _L0_rec_in["Wv_r"],
        "L0_rec_bv_r": _L0_rec_in["bv_r"],
        "L0_rec_Wv_i": _L0_rec_in["Wv_i"],
        "L0_rec_bv_i": _L0_rec_in["bv_i"],
        "L0_rec_Wo_r": _L0_rec_in["Wo_r"],
        "L0_rec_bo_r": _L0_rec_in["bo_r"],
        "L0_rec_Wo_i": _L0_rec_in["Wo_i"],
        "L0_rec_bo_i": _L0_rec_in["bo_i"],
        "L0_rec_int_Wr": _L0_rec_in["int_Wr"],
        "L0_rec_int_Wi": _L0_rec_in["int_Wi"],
        "L0_rec_meas_Mr": _L0_rec_in["meas_Mr"],
        "L0_rec_meas_Mi": _L0_rec_in["meas_Mi"],
        "L0_rec_post_W": _L0_rec_in["post_W"],
        "L0_rec_post_b": _L0_rec_in["post_b"],
        "L0_rec_post_g": _L0_rec_in["post_g"],
        "L0_rec_post_be": _L0_rec_in["post_be"],
    }

def reference(r_x, ids, tbl_0, tbl_1, tbl_2, tbl_3, W_top1, b_top1, W_top2, b_top2, W_top3, L0_rec_er_W1, L0_rec_er_b1, L0_rec_er_g1, L0_rec_er_be1, L0_rec_er_W2, L0_rec_er_b2, L0_rec_ei_W1, L0_rec_ei_b1, L0_rec_ei_g1, L0_rec_ei_be1, L0_rec_ei_W2, L0_rec_ei_b2, L0_rec_Wq_r, L0_rec_bq_r, L0_rec_Wq_i, L0_rec_bq_i, L0_rec_Wk_r, L0_rec_bk_r, L0_rec_Wk_i, L0_rec_bk_i, L0_rec_Wv_r, L0_rec_bv_r, L0_rec_Wv_i, L0_rec_bv_i, L0_rec_Wo_r, L0_rec_bo_r, L0_rec_Wo_i, L0_rec_bo_i, L0_rec_int_Wr, L0_rec_int_Wi, L0_rec_meas_Mr, L0_rec_meas_Mi, L0_rec_post_W, L0_rec_post_b, L0_rec_post_g, L0_rec_post_be):
    import jax
    import jax.numpy as jnp
    def _L0_rec_ref(x, strength, er_W1, er_b1, er_g1, er_be1, er_W2, er_b2, ei_W1, ei_b1, ei_g1, ei_be1, ei_W2, ei_b2, Wq_r, bq_r, Wq_i, bq_i, Wk_r, bk_r, Wk_i, bk_i, Wv_r, bv_r, Wv_i, bv_i, Wo_r, bo_r, Wo_i, bo_i, int_Wr, int_Wi, meas_Mr, meas_Mi, post_W, post_b, post_g, post_be):
        import jax, jax.numpy as jnp
        import numpy as np
        B, IN, HID, D, N, OUT = (4096, 2048, 2048, 512, 4, 512)
        H = 8
        HD = D // H

        def _ln(x, g, b):
            m = x.mean(-1, keepdims=True)
            v = ((x - m) ** 2).mean(-1, keepdims=True)
            return (x - m) / jnp.sqrt(v + 1e-05) * g + b
        Bsz = x.shape[0]

        def enc(W1, b1, g, be, W2, b2):
            h = jax.nn.gelu(_ln(x @ W1.T + b1, g, be), approximate=False)
            return (h @ W2.T + b2).reshape(Bsz, N, D)
        sr = enc(er_W1, er_b1, er_g1, er_be1, er_W2, er_b2)
        si = enc(ei_W1, ei_b1, ei_g1, ei_be1, ei_W2, ei_b2)

        def heads(t):
            return t.reshape(Bsz, N, H, HD).transpose(0, 2, 1, 3)
        qr = heads(sr @ Wq_r.T + bq_r)
        qi = heads(si @ Wq_i.T + bq_i)
        kr = heads(sr @ Wk_r.T + bk_r)
        ki = heads(si @ Wk_i.T + bk_i)
        vr = heads(sr @ Wv_r.T + bv_r)
        vi = heads(si @ Wv_i.T + bv_i)
        ar = jnp.einsum('bhnd,bhmd->bhnm', qr, kr) + jnp.einsum('bhnd,bhmd->bhnm', qi, ki)
        ai = jnp.einsum('bhnd,bhmd->bhnm', qi, kr) - jnp.einsum('bhnd,bhmd->bhnm', qr, ki)
        mag = jnp.sqrt(ar ** 2 + ai ** 2 + 1e-08) * HD ** (-0.5)
        w = jax.nn.softmax(mag, axis=-1)
        out_r = jnp.einsum('bhnm,bhmd->bhnd', w, vr).transpose(0, 2, 1, 3).reshape(Bsz, N, D)
        out_i = jnp.einsum('bhnm,bhmd->bhnd', w, vi).transpose(0, 2, 1, 3).reshape(Bsz, N, D)
        attn_r = out_r @ Wo_r.T + bo_r
        attn_i = out_i @ Wo_i.T + bo_i
        R = jnp.einsum('bnd,ned->bne', attn_r, int_Wr) - jnp.einsum('bnd,ned->bne', attn_i, int_Wi)
        I = jnp.einsum('bnd,ned->bne', attn_r, int_Wi) + jnp.einsum('bnd,ned->bne', attn_i, int_Wr)
        Ri, Ii = (R[:, :, None, :], I[:, :, None, :])
        Rj, Ij = (R[:, None, :, :], I[:, None, :, :])
        phase = jnp.arctan2(Ii * Rj - Ri * Ij, Ri * Rj + Ii * Ij)
        f = jnp.cos(phase) * strength[..., None]
        sup_r = jnp.einsum('bijd,bjd->bd', f, R)
        sup_i = jnp.einsum('bijd,bjd->bd', f, I)
        norm = jnp.sqrt(jnp.sum(sup_r ** 2 + sup_i ** 2, axis=-1, keepdims=True) + 1e-08)
        sup_r = sup_r / norm
        sup_i = sup_i / norm
        mr = sup_r @ meas_Mr.T - sup_i @ meas_Mi.T
        mi = sup_r @ meas_Mi.T + sup_i @ meas_Mr.T
        amp = jnp.sqrt(mr ** 2 + mi ** 2)
        out = jax.nn.gelu(_ln(amp @ post_W.T + post_b, post_g, post_be), approximate=False)
        return out

    e = jnp.stack([tbl_0[ids[:, 0]], tbl_1[ids[:, 1]], tbl_2[ids[:, 2]], tbl_3[ids[:, 3]]], axis=1)
    z = _L0_rec_ref(r_x, e, L0_rec_er_W1, L0_rec_er_b1, L0_rec_er_g1, L0_rec_er_be1, L0_rec_er_W2, L0_rec_er_b2, L0_rec_ei_W1, L0_rec_ei_b1, L0_rec_ei_g1, L0_rec_ei_be1, L0_rec_ei_W2, L0_rec_ei_b2, L0_rec_Wq_r, L0_rec_bq_r, L0_rec_Wq_i, L0_rec_bq_i, L0_rec_Wk_r, L0_rec_bk_r, L0_rec_Wk_i, L0_rec_bk_i, L0_rec_Wv_r, L0_rec_bv_r, L0_rec_Wv_i, L0_rec_bv_i, L0_rec_Wo_r, L0_rec_bo_r, L0_rec_Wo_i, L0_rec_bo_i, L0_rec_int_Wr, L0_rec_int_Wi, L0_rec_meas_Mr, L0_rec_meas_Mi, L0_rec_post_W, L0_rec_post_b, L0_rec_post_g, L0_rec_post_be)
    z = z.reshape(z.shape[0], -1)
    h = jnp.concatenate([z, r_x], axis=1)
    h = jnp.maximum(h @ W_top1 + b_top1, 0.0)
    h = jnp.maximum(h @ W_top2 + b_top2, 0.0)
    y = h @ W_top3
    return y


_drawn_inputs = setup_inputs


def setup_inputs(seed=0):
    import zlib

    import numpy as np

    out = dict(_drawn_inputs(seed))
    spreads = {'b_top1': (0.0, 0.1),
     'b_top2': (0.0, 0.1),
     'L0_rec_er_b1': (0.0, 0.8),
     'L0_rec_er_g1': (1.0, 0.6),
     'L0_rec_er_be1': (0.0, 0.8),
     'L0_rec_er_b2': (0.0, 0.8),
     'L0_rec_ei_b1': (0.0, 0.8),
     'L0_rec_ei_g1': (1.0, 0.6),
     'L0_rec_ei_be1': (0.0, 0.8),
     'L0_rec_ei_b2': (0.0, 0.8),
     'L0_rec_bq_r': (0.0, 0.8),
     'L0_rec_bq_i': (0.0, 0.8),
     'L0_rec_bk_r': (0.0, 0.8),
     'L0_rec_bk_i': (0.0, 0.8),
     'L0_rec_bv_r': (0.0, 0.1),
     'L0_rec_bv_i': (0.0, 0.1),
     'L0_rec_bo_r': (0.0, 0.1),
     'L0_rec_bo_i': (0.0, 0.1),
     'L0_rec_int_Wi': (0.0, 0.1),
     'L0_rec_post_b': (0.0, 0.1),
     'L0_rec_post_g': (1.0, 0.2),
     'L0_rec_post_be': (0.0, 0.1)}
    factors = {'L0_rec_Wq_r': 8.0, 'L0_rec_Wq_i': 8.0, 'L0_rec_Wk_r': 8.0, 'L0_rec_Wk_i': 8.0}
    for name, (base, spread) in spreads.items():
        noise = np.random.default_rng([zlib.crc32(name.encode()), seed]).standard_normal(out[name].shape)
        drawn = base * np.exp(spread * noise) if base else spread * noise
        out[name] = jnp.asarray(drawn.astype(out[name].dtype))
    for name, factor in factors.items():
        out[name] = (out[name] * factor).astype(out[name].dtype)
    return out
```

```python
from contextlib import ExitStack

import concourse.bass as bass
from concourse import mybir

F32 = mybir.dt.float32
F32R = mybir.dt.float32r
I32 = mybir.dt.int32
ACT = mybir.ActivationFunctionType
ALU = mybir.AluOpType
AX = mybir.AxisListType

P = 128
LN_EXP_SET = 6
SCRATCH = "Internal"
B, IN, HID, D, N, OUT = 1024, 2048, 2048, 512, 4, 512
H = 8
HD = D // H
KC = IN // P
DC = D // P
HALF = B // 2
BLK = KC * P

COLS = {}
_at = 0
for _name, _n in (("b1_r", KC), ("b1_i", KC), ("b_top1", DC), ("b2_r", KC), ("b2_i", KC),
                  ("g_r", KC), ("be_r", KC), ("g_i", KC), ("be_i", KC),
                  ("bqkv_r", 3 * DC), ("bqkv_i", 3 * DC), ("bo_r", DC), ("bo_i", DC),
                  ("post_b", DC), ("post_g", DC), ("post_be", DC), ("b_top2", 2), ("w_top3", 2)):
    COLS[_name] = _at
    _at += _n
NCOLS = _at

G_L1 = {"r": 0, "i": KC}
G_TOP = 2 * KC
G_L2 = {"r": G_TOP + DC, "i": G_TOP + DC + KC}
G_END = G_L2["i"] + KC
G_WO = G_END + 6 * 2
GROUPS = B * N // P
TILES_B = B // P
HU = H // 2
TILES_Q = 3 * DC * 2 * N


def build(nc, xT, ids, tbl, w, cols, y):
    hT = {s: nc.dram_tensor(f"hT_{s}", [KC, P, B], F32, kind=SCRATCH).ap() for s in "ri"}
    sT = {s: nc.dram_tensor(f"sT_{s}", [KC, P, B], F32, kind=SCRATCH).ap() for s in "ri"}
    topT = nc.dram_tensor("topT", [DC, P, B], F32, kind=SCRATCH).ap()
    stat_rows = nc.dram_tensor("stat_rows", [1, 2 * B], F32, kind=SCRATCH).ap()
    qkvT = {s: nc.dram_tensor(f"qkvT_{s}", [3, D, B * N], F32, kind=SCRATCH).ap() for s in "ri"}

    attnT = {s: nc.dram_tensor(f"attnT_{s}", [DC, P, N, B], F32, kind=SCRATCH).ap() for s in "ri"}

    supT = nc.dram_tensor("supT", [2, DC, P, B], F32, kind=SCRATCH).ap()

    ctx = ExitStack()
    with ctx:
        def sb(name, shape, dt=F32):
            return ctx.enter_context(nc.sbuf_tensor(name, shape, dt))

        def sem(name):
            return ctx.enter_context(nc.semaphore(name))

        act_hi = sb("act_hi", [P, KC, B], F32R)
        act_lo = sb("act_lo", [P, KC, B], F32R)
        w_hi = sb("w_hi", [P, 2, BLK], F32R)
        w_lo = sb("w_lo", [P, 2, BLK], F32R)
        arena = sb("arena", [P, 11264])
        par = sb("par", [P, NCOLS])
        ones = sb("ones", [P, P])

        w_raw = arena[:, 0:BLK]
        ring = [arena[:, 2048 + 1024 * i:2048 + 1024 * (i + 1)] for i in range(3)]
        misc = [arena[:, 5120 + 2048 * i:5120 + 2048 * (i + 1)] for i in range(3)]
        hout = [misc[0][:, 0:B], misc[0][:, B:2 * B]]
        acc, acc2 = misc[1][:, 0:B], misc[1][:, B:2 * B]
        st = misc[2]
        sq = ring[2]
        qout = [m.rearrange("p (b n) -> p b n", n=N) for m in misc[:2]]

        ps = [ctx.enter_context(nc.psum_tensor(f"ps{i}", [P, B], F32)) for i in range(2)]
        ps_st = [ctx.enter_context(nc.psum_tensor(f"ps_st{i}", [P, B], F32)) for i in range(2)]

        zero = sb("zero", [P, 1])
        ident = sb("ident", [P, P])
        same_row = sb("same_row", [P, P])
        same_row32 = sb("same_row32", [P, 32])
        v_raw = arena[:, 0:1024].rearrange("p (s c x) -> p s c x", s=2, c=DC)
        wi_raw = arena[:, 1024:2048]
        qk = [arena[:, 2048 + 1536 * i:2048 + 1536 * (i + 1)] for i in range(2)]
        q_u = [x[:, 0:512].rearrange("p (h x) -> p h x", h=HU) for x in qk]
        kk_u = [x[:, 512:1536].rearrange("p (h e x) -> p h e x", h=HU, e=2) for x in qk]
        z_w = [arena[:, 5120 + 1024 * i:5120 + 1024 * (i + 1)].rearrange("p (h x) -> p h x", h=H)
               for i in range(2)]
        wT = arena[:, 7168:8192].rearrange("p (h x) -> p h x", h=H)
        a_out = [arena[:, 8192 + 512 * i:8192 + 512 * (i + 1)] for i in range(2)]
        sc = [arena[:, 9216 + 256 * i:9216 + 256 * (i + 1)].rearrange("p (a x) -> p a x", x=32) for i in range(2)]
        small = arena[:, 9728:10240]
        ar = small[:, 0:64]
        ar_sq = small[:, 64:128]
        mag = small[:, 128:160].rearrange("p (h m) -> p h m", m=N)
        top = small[:, 160:168]
        ex = small[:, 192:224].rearrange("p (h m) -> p h m", m=N)
        total = small[:, 224:232]
        inv = small[:, 232:240]
        wgt = small[:, 240:272].rearrange("p (h m) -> p h m", m=N)
        v_nat = arena[:, 10240:11264].rearrange("p (s x) -> p s x", s=2)

        par_in = sem("par_in")
        w_in = sem("w_in")
        w_hi_done = sem("w_hi_done")
        w_lo_done = sem("w_lo_done")
        raw_in = [sem(f"raw_in{i}") for i in range(3)]
        cent = sem("cent")
        normed = sem("normed")
        gelu_done = sem("gelu_done")
        act_hi_done = sem("act_hi_done")
        act_lo_done = sem("act_lo_done")
        used = sem("used")
        evac = sem("evac")
        tile_done = sem("tile_done")
        tile_evac = sem("tile_evac")
        stored = [sem(f"stored{i}") for i in range(2)]
        acc_done = sem("acc_done")
        sq_done = sem("sq_done")
        acc2_done = sem("acc2_done")
        ones_done = sem("ones_done")
        zeroed = sem("zeroed")
        sums_done = sem("sums_done")
        st_mean = sem("st_mean")
        st_msq = sem("st_msq")
        st_var = sem("st_var")
        st_eps = sem("st_eps")
        st_root = sem("st_root")
        st_recip = sem("st_recip")
        st_saved = sem("st_saved")
        st_back = sem("st_back")
        q_stored = [sem(f"q_stored{i}") for i in range(2)]

        ident_z = sem("ident_z")
        masks = sem("masks")
        v_in = sem("v_in")
        qk_in = [sem(f"qk_in{i}") for i in range(2)]
        negated = sem("negated")
        scores_done = sem("scores_done")
        diag_done = sem("diag_done")
        masked = sem("masked")
        ar_done = sem("ar_done")
        ar_sq_done = sem("ar_sq_done")
        mag2_done = sem("mag2_done")
        mag_done = sem("mag_done")
        top_done = sem("top_done")
        diff_done = sem("diff_done")
        exp_done = sem("exp_done")
        total_done = sem("total_done")
        inv_done = sem("inv_done")
        wgt_done = sem("wgt_done")
        z_done = sem("z_done")
        vT_done = sem("vT_done")
        v_nat_done = sem("v_nat_done")
        zT_done = sem("zT_done")
        wT_done = sem("wT_done")
        pv_done = sem("pv_done")
        o_hi_done = sem("o_hi_done")
        o_lo_done = sem("o_lo_done")
        wo_done = sem("wo_done")
        a_out_done = sem("a_out_done")
        a_stored = [sem(f"a_stored{i}") for i in range(2)]

        WI_FIRST = {1: [0], 2: [1], 3: [2, 3, 4]}
        WI_LOOP = 5
        wi_in = sem("wi_in")
        wi_hi_done = sem("wi_hi_done")
        wi_lo_done = sem("wi_lo_done")

        z = arena[:, 0:4096].rearrange("p (q e n x) -> p q e n x", q=4, e=2, n=N)
        a_raw = arena[:, 4096:5120].rearrange("p (s c x) -> p s c x", s=2, c=DC)
        z_sq = [arena[:, 5120 + 512 * i:6144 + 512 * i].rearrange("p (e n x) -> p e n x", e=2, n=N)
                for i in range(2)]
        m2 = [z_sq[0][:, 0], z_sq[1][:, 1]]
        rt = [arena[:, 6656 + 512 * i:7168 + 512 * i].rearrange("p (n x) -> p n x", n=N) for i in range(2)]
        un = arena[:, 7680:8704].rearrange("p (e n x) -> p e n x", e=2, n=N)
        t_r = arena[:, 8704:9472].rearrange("p (k x) -> p k x", k=6)
        t_i = arena[:, 9472:10240].rearrange("p (k x) -> p k x", k=6)
        sup = arena[:, 10240:11264].rearrange("p (e x) -> p e x", e=2)
        sup_flat = arena[:, 10240:11264]
        PAIRS = [(i, i + d) for d in range(1, N) for i in range(N - d)]
        AT = {1: (0, 3), 2: (3, 5), 3: (5, 6)}
        nrm = sb("nrm", [P, 2])
        tiny = sb("tiny", [P, 2])
        ids_sb = sb("ids_sb", [P, TILES_B, N], I32)
        strength = sb("strength", [P, TILES_B, N * N])
        ids_in = sem("ids_in")
        strength_in = sem("strength_in")
        a_in = sem("a_in")
        a_hi_done = sem("a_hi_done")
        a_lo_done = sem("a_lo_done")
        neg_lo_done = sem("neg_lo_done")
        int_done = sem("int_done")
        z_out = sem("z_out")
        z_sq_done = sem("z_sq_done")
        m2_done = sem("m2_done")
        ln_done = sem("ln_done")
        rinv_done = sem("rinv_done")
        ur_done = sem("ur_done")
        ui_done = sem("ui_done")
        tr_done = sem("tr_done")
        ti_done = sem("ti_done")
        t_done = sem("t_done")
        zero_marked = sem("zero_marked")
        t_first = sem("t_first")
        t_marked = sem("t_marked")
        t_mult = sem("t_mult")
        c_round = sem("c_round")
        prod_done = sem("prod_done")
        half_sum = sem("half_sum")
        sup_done = sem("sup_done")
        nrm_sq = sem("nrm_sq")
        nrm_ln = sem("nrm_ln")
        nrm_inv = sem("nrm_inv")
        scaled = sem("scaled")
        supT_done = sem("supT_done")
        supT_out = sem("supT_out")
        sup_stored = sem("sup_stored")

        mr_st = [arena[:, 2048 + 1024 * i:3072 + 1024 * i] for i in range(2)]
        top_x = [arena[:, 4096 + 512 * i:4608 + 512 * i] for i in range(2)]
        post = arena[:, 5120:9216].rearrange("p (c x) -> p c x", c=DC)
        m_sq = arena[:, 9216:10240]
        x_t = [arena[:, 10240 + 512 * i:10752 + 512 * i] for i in range(2)]
        post_sq = arena[:, 9216:11264].rearrange("p (c x) -> p c x", c=DC)
        top_in = [sem(f"top_in{i}") for i in range(2)]
        meas_done = sem("meas_done")
        m_sq_done = sem("m_sq_done")
        amp2_done = sem("amp2_done")
        amp_done = sem("amp_done")
        amp_hi_done = sem("amp_hi_done")
        amp_lo_done = sem("amp_lo_done")
        post_done = sem("post_done")
        post_out = sem("post_out")
        post_sq_done = sem("post_sq_done")
        post_sums = sem("post_sums")
        p_mean = sem("p_mean")
        p_msq = sem("p_msq")
        p_var = sem("p_var")
        p_eps = sem("p_eps")
        p_root = sem("p_root")
        p_inv = sem("p_inv")
        p_cent = sem("p_cent")
        p_normed = sem("p_normed")
        z_gelu = sem("z_gelu")
        z_hi_done = sem("z_hi_done")
        z_lo_done = sem("z_lo_done")
        top1_done = sem("top1_done")
        x_done = sem("x_done")
        h1_hi_done = sem("h1_hi_done")
        h1_lo_done = sem("h1_lo_done")
        top2_done = sem("top2_done")
        h2_done = sem("h2_done")
        y_done = sem("y_done")
        y_out = sem("y_out")
        y_stored = sem("y_stored")

        def acc_at(mt):
            return ps_st[mt // 2][:, (mt % 2) * 512:(mt % 2 + 1) * 512]

        def cols_of(half):
            return slice(half * HALF, (half + 1) * HALF)

        SETS = ["x", "h_r", "h_i", "s_r", "s_i"]
        SRC = {"x": xT, "h_r": hT["r"], "h_i": hT["i"], "s_r": sT["r"], "s_i": sT["i"]}
        LAST = {1: G_TOP + DC - 1, 2: G_L2["r"] + KC - 1, 3: G_L2["i"] + KC - 1}
        STAGES = [("l1_r", 0, KC), ("l1_i", KC, KC), ("top1x", G_TOP, DC), ("l2_r", G_L2["r"], KC),
                  ("l2_i", G_L2["i"], KC)]
        BIAS = {"l1_r": "b1_r", "l1_i": "b1_i", "top1x": "b_top1", "l2_r": "b2_r", "l2_i": "b2_i"}
        OUTS = {"l1_r": hT["r"], "l1_i": hT["i"], "top1x": topT, "l2_r": sT["r"], "l2_i": sT["i"]}
        NEXT_SET = {"top1x": 1, "l2_r": 2, "l2_i": 3}

        def blocks(eng, stage, step):
            name, g0, n = stage
            lo, hi = g0 // 2, (g0 + n) // 2
            first = lo + (name in ("l1_r", "l1_i", "top1x", "l2_r", "l2_i"))
            last = hi - (name in NEXT_SET)
            for j in range(lo, first):
                for p in range(2):
                    step(j, p)
            if first < last:
                with eng.Fori(first, last) as j:
                    for p in range(2):
                        step(j, p)
            for j in range(max(last, first), hi):
                for p in range(2):
                    step(j, p)

        def is_block(j, p, g):
            return isinstance(j, int) and 2 * j + p == g

        def wait_chunk_free(eng, k, c):
            if k in LAST:
                eng.wait_ge(used, KC * LAST[k] + c + 1)
            if k == 4:
                eng.wait_ge(tile_done, TILES_Q - N + c // DC + 1)

        def groups(eng, step):
            for g in range(4):
                step(0, g)
            with eng.Fori(1, TILES_B) as t:
                for g in range(4):
                    step(t, g)
            for g in range(2):
                step(TILES_B, g)

        def tiles(eng, step):
            step(0)
            with eng.Fori(1, TILES_B - 2) as t:
                step(t)
            step(TILES_B - 2)
            step(TILES_B - 1)

        block = ctx.enter_context(nc.Block())

        @block.sync
        def _(sp):
            sp.dma_start(par[:, :], cols).then_inc(par_in, 16)

            def weights(src, g):
                sp.wait_ge(w_lo_done, g)
                sp.dma_start(w_raw, src).then_inc(w_in, 16)

            def chunks(k):
                if k == 1:
                    sp.wait_ge(sums_done, 2)
                    sp.wait_ge(st_saved, 16)
                    sp.dma_start(misc[1], stat_rows.to_broadcast([P, 2 * B])).then_inc(st_back, 16)
                    sp.wait_ge(acc2_done, 2 * KC)
                if k in (1, 3):
                    for s in range(2):
                        sp.wait_ge(stored[s], 8 * (G_TOP if k == 1 else G_L2["i"]))
                if k in (2, 4):
                    for s in range(2):
                        sp.wait_ge(stored[s], 8 * (G_TOP if k == 2 else G_END))
                for c in range(KC):
                    q = KC * k + c
                    if q >= 3:
                        sp.wait_ge(act_lo_done, q - 2)
                    sp.dma_start(ring[q % 3], SRC[SETS[k]][c]).then_inc(raw_in[q % 3], 16)

            def stage(name, g0, n, k=None):
                weights(w[name][0], g0)
                if k is not None:
                    chunks(k)
                with sp.Fori(1, n) as m:
                    weights(w[name][m], m + g0)

            stage(*STAGES[0], 0)
            stage(*STAGES[1])
            stage(*STAGES[2])
            stage(*STAGES[3], 1)
            stage(*STAGES[4], 2)

            def half_blocks(s, k):
                u0 = 0 if s == "r" else 6

                def half_block(u, m, e):
                    sp.wait_ge(w_lo_done, G_END + u)
                    sp.dma_start(w_raw[:, 0:BLK // 2],
                                 w["qkv_" + s][m, :, e * (BLK // 2):(e + 1) * (BLK // 2)]).then_inc(w_in, 16)

                half_block(u0, 0, 0)
                chunks(k)
                half_block(u0 + 1, 0, 1)
                with sp.Fori(1, 3) as m:
                    for e in range(2):
                        half_block(2 * m + (u0 + e), m, e)

            half_blocks("r", 3)
            half_blocks("i", 4)

            for s in range(2):
                sp.wait_ge(w_lo_done, G_WO + s)
                sp.dma_start(w_raw, w["o"][s]).then_inc(w_in, 16)

            def load_unit(t, g, hh):
                e = hh
                if not (isinstance(t, int) and t == 0 and g == 0):
                    sp.wait_ge(scores_done, 8 * t + (2 * g + hh - 1))
                cs = bass.ds((t * 4 + g) * P, P)
                hs = slice(hh * HU, (hh + 1) * HU)
                for dst, m, s, lo in ((q_u[e], 0, "r", 0), (q_u[e], 0, "i", 64), (kk_u[e][:, :, 0], 1, "r", 0),
                                      (kk_u[e][:, :, 0], 1, "i", 64), (kk_u[e][:, :, 1], 1, "i", 0),
                                      (kk_u[e][:, :, 1], 1, "r", 64)):
                    src = qkvT[s][m].rearrange("(h d) x -> d h x", d=HD)[:, hs, cs]
                    sp.dma_start(dst[lo:lo + 64], src).then_inc(qk_in[e], 16)

            def load_v(t, g):
                if not (isinstance(t, int) and 4 * t + g == 0):
                    sp.wait_ge(vT_done, 8 * t + 2 * g)
                for si, s in enumerate("ri"):
                    src = qkvT[s][2].rearrange("(c p) x -> p c x", p=P)[:, :, bass.ds((t * 4 + g) * P, P)]
                    sp.dma_start(v_raw[:, si], src).then_inc(v_in, 16)

            def load_wi(b):
                sp.wait_ge(wi_lo_done, b)
                sp.dma_start(wi_raw, w["int"][b]).then_inc(wi_in, 16)

            sp.wait_ge(act_lo_done, 5 * KC)
            for half in range(2):
                sp.wait_ge(q_stored[half], 16 * 3 * DC * 2)

            def step(t, g):
                first = isinstance(t, int) and t == 0
                if not (isinstance(t, int) and t == TILES_B):
                    for hh in range(2):
                        load_unit(t, g, hh)
                if first and g == 1:
                    sp.wait_ge(w_lo_done, G_WO + 2)
                if not (first and g == 0 or isinstance(t, int) and t == TILES_B and g == 1):
                    load_v(t, g - 1)
                if first and g > 0:
                    for b in WI_FIRST[g]:
                        load_wi(b)
                if not isinstance(t, int) and g == 1:
                    load_wi(t + (WI_LOOP - 1))

            groups(sp, step)

            for b in range(12, 16):
                load_wi(b)
            for e in range(2):
                sp.wait_ge(a_stored[e], 16 * DC * TILES_B)

            def load_a(t, pos, bs):
                n = (pos + 1) % N
                if t or pos:
                    sp.wait_ge(a_lo_done, 4 * t + pos)
                    sp.wait_ge(neg_lo_done, 4 * t + pos)
                for si, s in enumerate("ri"):
                    src = attnT[s].rearrange("c p n b -> p n c b")[:, n, :, bs]
                    sp.dma_start(a_raw[:, si], src).then_inc(a_in, 16)

            for t in range(TILES_B):
                bs = slice(t * P, (t + 1) * P)
                for pos in range(N):
                    load_a(t, pos, bs)

            sp.wait_ge(sup_stored, 32 * TILES_B)
            for k, src in enumerate((w["meas"][0], w["meas"][1], w["post"], w["top1z"], w["top2"])):
                if k < 2:
                    sp.wait_ge(w_lo_done, G_WO + 2 + k)
                    sp.dma_start(w_raw, src).then_inc(w_in, 16)
                if k == 1:
                    for c in range(2 * DC):
                        q = 5 * KC + c
                        if c >= 3:
                            sp.wait_ge(act_lo_done, q - 2)
                        sp.dma_start(ring[q % 3], supT[c // DC][c % DC]).then_inc(raw_in[q % 3], 16)
                if k >= 2:
                    sp.wait_ge(w_lo_done, G_WO + 2 + k)
                    sp.dma_start(w_raw[:, 0:src.shape[1]], src).then_inc(w_in, 16)
            sp.wait_ge(act_lo_done, 5 * KC + 2 * DC)
            for u in range(2 * DC):
                if u >= 2:
                    sp.wait_ge(x_done, u - 1)
                half, mt = u // DC, u % DC
                sp.dma_start(top_x[u % 2], topT[mt][:, half * HALF:(half + 1) * HALF]).then_inc(top_in[u % 2], 16)

        @block.scalar
        def _(act):
            act.wait_ge(par_in, 16)

            def split(j, p):
                act.wait_ge(w_in, 32 * j + 16 * p + 16)
                if not (isinstance(j, int) and j == 0):
                    act.wait_ge(used, 2 * KC * j + KC * (p - 1))
                act.activation(w_hi[:, p, :], w_raw, ACT.Copy).then_inc(w_hi_done, 1)

            def chunks(k, some=range(KC)):
                name = SETS[k]
                for c in some:
                    q = KC * k + c
                    if name[0] == "h":
                        act.wait_ge(normed, KC * (k - 1) + c + 1)
                        g0, b0 = COLS["g_" + name[2]] + c, COLS["be_" + name[2]] + c
                        act.activation(ring[q % 3], ring[q % 3], ACT.Gelu, bias=par[:, b0:b0 + 1],
                                       scale=par[:, g0:g0 + 1]).then_inc(gelu_done, 1)
                        act.wait_ge(gelu_done, KC * (k - 1) + c + 1)
                    else:
                        act.wait_ge(raw_in[q % 3], 16 * (q // 3 + 1))
                    wait_chunk_free(act, k, c)
                    act.activation(act_hi[:, c, :], ring[q % 3], ACT.Copy).then_inc(act_hi_done, 1)

            def take_out(j, p, name, g0):
                act.wait_ge(used, 2 * KC * j + KC * (p + 1))
                if not (isinstance(j, int) and j == 0):
                    act.wait_ge(stored[p], 16 * j)
                    if name in ("l1_r", "l1_i"):
                        act.wait_ge(acc_done, 2 * j + p - 1)
                        act.wait_ge(acc2_done, 2 * j + p - 1)
                    if name == "top1x":
                        act.wait_ge(acc_done, 2 * KC)
                        act.wait_ge(acc2_done, 2 * KC)
                act.activation(hout[p], ps[p][:, :], ACT.Identity,
                               bias=par[:, bass.ds(2 * j + (p + COLS[BIAS[name]] - g0), 1)]).then_inc(evac, 1)

            def half_block_split(u, e, tiles=None):
                act.wait_ge(w_in, 16 * u + 16 * G_END + 16)
                if tiles is None:
                    act.wait_ge(used, KC * (G_END - (1 - e)))
                else:
                    act.wait_ge(tile_done, tiles)
                act.activation(w_hi[:, e, 0:BLK // 2], w_raw[:, 0:BLK // 2], ACT.Copy).then_inc(w_hi_done, 1)

            split(0, 0)
            chunks(0)
            for stage in STAGES:
                name, g0, n = stage

                def step(j, p):
                    if is_block(j, p, G_END - 1):
                        half_block_split(0, 0)
                    elif p == 0:
                        split(j, 1)
                    else:
                        split(j + 1, 0)
                    if name in NEXT_SET and is_block(j, p, g0 + n - 1):
                        chunks(NEXT_SET[name])
                    take_out(j, p, name, g0)
                    if is_block(j, p, KC) or is_block(j, p, G_TOP):
                        act.wait_ge(st_eps, 1 + (g0 == G_TOP))
                        act.activation(st[:, B:2 * B], st[:, B:2 * B], ACT.Sqrt).then_inc(st_root, 1)

                blocks(act, stage, step)

            for s in range(2):
                act.wait_ge(stored[s], 8 * G_END)
            for si, s in enumerate("ri"):
                T0 = TILES_Q * si

                def tile(m, mt, half, n):
                    i = (mt * 2 + half) * N + n
                    u = 2 * N * DC * m + (T0 + i)
                    act.wait_ge(tile_done, u + 1)
                    if n == 0:
                        act.wait_ge(q_stored[half], 16 * DC * m + 16 * (DC * 3 * si + mt))
                    c0 = COLS["bqkv_" + s] + mt
                    act.activation(qout[half][:, :, n], ps_st[i // 2 % 2][:, (i % 2) * HALF:(i % 2 + 1) * HALF],
                                   ACT.Identity, bias=par[:, bass.ds(DC * m + c0, 1)]).then_inc(tile_evac, 1)

                def half_tiles(m, e, then_chunks=False):
                    for mt in range(2 * e, 2 * e + 2):
                        for half in range(2):
                            for n in range(N):
                                tile(m, mt, half, n)
                                if then_chunks and mt == DC - 1 and half == 1:
                                    chunks(4, range(n * DC, (n + 1) * DC))

                def matrix(m, last):
                    if isinstance(m, int) and m == 0 and si == 0:
                        half_block_split(1, 1)
                    else:
                        half_block_split(2 * m + (6 * si + 1), 1, 32 * m + T0)
                    half_tiles(m, 0)
                    if not last:
                        half_block_split(2 * m + (6 * si + 2), 0, 32 * m + (T0 + 16))
                    elif si == 0:
                        half_block_split(6, 0, T0 + 80)
                    half_tiles(m, 1, last and si == 0)

                matrix(0, False)
                matrix(1, False)
                matrix(2, True)

            act.wait_ge(tile_done, 2 * TILES_Q)
            for s in range(2):
                act.wait_ge(w_in, 16 * (G_WO + s + 1))
                act.activation(w_hi[:, s, :], w_raw, ACT.Copy).then_inc(w_hi_done, 1)
            for half in range(2):
                act.wait_ge(q_stored[half], 16 * 3 * DC * 2)

            def split_wi(b, at=None):
                act.wait_ge(wi_in, 16 * b + 16)
                dst = act_hi[:, b + DC, :] if at is None else act_hi[:, at, :]
                act.activation(dst, wi_raw, ACT.Copy).then_inc(wi_hi_done, 1)

            def step(t, g):
                start, end = isinstance(t, int) and t == 0, isinstance(t, int) and t == TILES_B
                k1 = 4 * t + (g - 1)
                if not (start and g < 2):
                    for si in range(2):
                        act.wait_ge(vT_done, 2 * k1 + (si - 1))
                        if not (start and g == 2):
                            act.wait_ge(pv_done, 2 * k1 - 2)
                        act.activation(v_nat[:, si], ps_st[0][:, si * 512:(si + 1) * 512],
                                       ACT.Copy).then_inc(v_nat_done, 1)
                if not end:
                    for hh in range(2):
                        act.wait_ge(scores_done, 8 * t + (2 * g + hh + 1))
                        if not (start and g == 0):
                            act.wait_ge(ar_done, 8 * t + (2 * g + hh - 1))
                        src = ps[hh][:, :].rearrange("p (a x) -> p a x", x=P)
                        for qd in range(4):
                            rows = slice(32 * qd, 32 * qd + 32)
                            act.activation(sc[hh][rows], src[rows, :, rows], ACT.Copy).then_inc(diag_done, 1)
                if not (start and g < 2):
                    for si in range(2):
                        act.wait_ge(pv_done, 2 * k1 + (si - 1))
                        if g == 2 and not start:
                            act.wait_ge(wo_done, 8 * t)
                        cs = slice((g + 2) % 4 * P, ((g + 2) % 4 + 1) * P)
                        act.activation(act_hi[:, 0:DC, si * HALF + cs.start:si * HALF + cs.stop],
                                       ps_st[1][:, si * 512:(si + 1) * 512].rearrange("p (c x) -> p c x", c=DC),
                                       ACT.Copy).then_inc(o_hi_done, 1)
                if not end:
                    act.wait_ge(mag2_done, 4 * t + (g + 1))
                    act.activation(mag, mag, ACT.Sqrt).then_inc(mag_done, 1)
                    act.wait_ge(diff_done, 4 * t + (g + 1))
                    act.activation(ex, ex, ACT.Exp, scale=HD ** -0.5).then_inc(exp_done, 1)
                if g == 1 and not start:
                    for i in range(2 * DC):
                        act.wait_ge(wo_done, 8 * t + (i - 7))
                        if i >= 2 or not (isinstance(t, int) and t == 1):
                            act.wait_ge(a_stored[i % 2], 64 * t + (16 * (i // 2) - 64))
                        c0 = COLS["bo_" + "ri"[i // DC]] + i % DC
                        act.activation(a_out[i % 2].rearrange("p (n b) -> p b n", n=N),
                                       ps_st[0][:, (i % 2) * 512:(i % 2 + 1) * 512]
                                       .rearrange("p (b n) -> p b n", n=N), ACT.Identity,
                                       bias=par[:, c0:c0 + 1]).then_inc(a_out_done, 1)
                        act.wait_ge(a_out_done, 8 * t + (i - 7))
                        act.dma_start(attnT["ri"[i // DC]][i % DC][:, :, bass.ds((t - 1) * P, P)],
                                      a_out[i % 2].rearrange("p (n b) -> p n b", n=N)).then_inc(a_stored[i % 2], 16)
                if start and g > 0:
                    for b in WI_FIRST[g]:
                        split_wi(b)
                if not isinstance(t, int) and g == 1:
                    split_wi(t + (WI_LOOP - 1))

            groups(act, step)

            act.add_instruction(mybir.InstLoadActFuncSet(name=nc.get_next_instruction_name(),
                                                         act_func_set_id=LN_EXP_SET, engine=act.engine))
            act.wait_ge(wo_done, 2 * DC * TILES_B)
            for b in range(12, 16):
                split_wi(b, b - 12)

            def split_a(t, pos):
                e = pos % 2
                act.wait_ge(a_in, 128 * t + 32 * (pos + 1))
                if not (isinstance(t, int) and t == 0 and pos < 2):
                    act.wait_ge(int_done, 4 * t + (pos - 1))
                act.activation(w_hi[:, e, 0:1024], a_raw.rearrange("p s c x -> p (s c x)"),
                               ACT.Copy).then_inc(a_hi_done, 1)
                act.activation(w_hi[:, e, 1024:1536], a_raw[:, 1].rearrange("p c x -> p (c x)"),
                               ACT.Copy, scale=-1.0).then_inc(a_hi_done, 1)

            def take_z(t, pos, quarters):
                lo, hi = quarters
                acc_ri = acc_of[pos].rearrange("p (e q x) -> p q e x", e=2, q=4)
                act.activation(z[:, lo:hi, :, (pos + 1) % N, :], acc_ri[:, lo:hi], ACT.Copy).then_inc(z_out, 1)

            def square(t, q):
                act.wait_ge(z_out, 8 * t + (8 if q == 3 else 4))
                if not (isinstance(t, int) and 4 * t + q == 0):
                    act.wait_ge(m2_done, 4 * t + q)
                if not (isinstance(t, int) and 4 * t + q < 2):
                    act.wait_ge(t_marked, 4 * t + (q - 1))
                    act.wait_ge(ti_done, 4 * t + (q - 1))
                act.activation(z_sq[q % 2], z[:, q], ACT.Square).then_inc(z_sq_done, 1)

            def one_over(t, q):
                Q1 = 4 * t + (q + 1)
                act.wait_ge(m2_done, Q1)
                if not (isinstance(t, int) and 4 * t + q < 2):
                    act.wait_ge(prod_done, Q1 - 2)
                act.activation(rt[q % 2], m2[q % 2], ACT.Ln, bias=tiny[:, 0:1]).then_inc(ln_done, 1)
                act.wait_ge(ln_done, Q1)
                act.activation(rt[q % 2], rt[q % 2], ACT.Exp, scale=-0.5).then_inc(rinv_done, 1)

            def norm(t1):
                act.wait_ge(sup_done, 4 * t1)
                act.wait_ge(m2_done, 4 * t1)
                act.activation(z_sq[1].rearrange("p e n x -> p (e n x)"), sup_flat, ACT.Square,
                               accum_out=nrm[:, 0:1]).then_inc(nrm_sq, 1)
                act.wait_ge(nrm_sq, t1)
                act.activation(nrm[:, 0:1], nrm[:, 0:1], ACT.Ln, bias=tiny[:, 1:2]).then_inc(nrm_ln, 1)
                act.wait_ge(nrm_ln, t1)
                if not (isinstance(t1, int) and t1 == 1):
                    act.wait_ge(scaled, t1 - 1)
                act.activation(nrm[:, 1:2], nrm[:, 0:1], ACT.Exp, scale=-0.5).then_inc(nrm_inv, 1)

            def store_sup(t1):
                for e in range(2):
                    act.wait_ge(supT_done, 2 * t1 + (e - 1))
                    if e == 0:
                        act.wait_ge(supT_done, 2 * t1)
                    act.activation(sup[:, e], ps_st[1][:, e * 512:(e + 1) * 512],
                                   ACT.Copy).then_inc(supT_out, 1)
                    act.wait_ge(supT_out, 2 * t1 + (e - 1))
                    act.dma_start(supT[e].rearrange("c p b -> p c b")[:, :, bass.ds((t1 - 1) * P, P)],
                                  sup[:, e].rearrange("p (c x) -> p c x", c=DC)).then_inc(sup_stored, 16)

            acc_of = [ps[0][:, :], ps[1][:, :], ps_st[0][:, :], ps_st[1][:, :]]
            for t, pos in [(0, 0), (0, 1), (0, 2), (0, 3), (1, 0)]:
                split_a(t, pos)
            act.wait_ge(wi_lo_done, 16)

            def step(t):
                start, last = isinstance(t, int) and t == 0, isinstance(t, int) and t == TILES_B - 1
                if not start:
                    act.wait_ge(sup_done, 4 * t - 1)
                for pos in range(N):
                    act.wait_ge(int_done, 4 * t + (pos + 1))
                    take_z(t, pos, (0, 3))
                square(t, 0)
                if not start:
                    act.wait_ge(sup_done, 4 * t)
                for pos in range(N):
                    take_z(t, pos, (3, 4))
                one_over(t, 0)
                if not last:
                    split_a(t + 1, 1)
                if not start:
                    norm(t)
                square(t, 1)
                one_over(t, 1)
                square(t, 2)
                one_over(t, 2)
                if not last:
                    split_a(t + 1, 2)
                if not start:
                    store_sup(t)
                square(t, 3)
                one_over(t, 3)
                if not last:
                    split_a(t + 1, 3)
                if not (isinstance(t, int) and t >= TILES_B - 2):
                    split_a(t + 2, 0)

            tiles(act, step)
            norm(TILES_B)
            store_sup(TILES_B)
            act.wait_ge(sup_stored, 32 * TILES_B)

            def split_w(k, e, n=BLK):
                act.wait_ge(w_in, 16 * (G_WO + 3 + k))
                act.activation(w_hi[:, e, 0:n], w_raw[:, 0:n], ACT.Copy).then_inc(w_hi_done, 1)

            act.wait_ge(int_done, N * TILES_B)
            split_w(0, 0)
            split_w(1, 1)
            for c in range(2 * DC):
                q = 5 * KC + c
                act.wait_ge(raw_in[q % 3], 16 * (q // 3 + 1))
                if c >= DC:
                    act.activation(act_hi[:, c + DC, :], ring[q % 3], ACT.Copy, scale=-1.0)
                act.activation(act_hi[:, c, :], ring[q % 3], ACT.Copy).then_inc(act_hi_done, 1)

            for u in range(2 * DC):
                half, mt = u // DC, u % DC
                act.wait_ge(meas_done, u + 1)
                if u:
                    act.wait_ge(amp2_done, u)
                act.activation(m_sq, ps[u % 2][:, :], ACT.Square).then_inc(m_sq_done, 1)
                act.wait_ge(amp2_done, u + 1)
                act.activation(x_t[u % 2], x_t[u % 2], ACT.Sqrt).then_inc(amp_done, 1)
                act.wait_ge(amp_done, u + 1)
                act.activation(act_hi[:, 3 * DC + mt, cols_of(half)], x_t[u % 2], ACT.Copy).then_inc(amp_hi_done, 1)
            split_w(2, 0)
            act.wait_ge(amp_lo_done, 2 * DC)
            for half in range(2):
                for mt in range(DC):
                    u = half * DC + mt
                    act.wait_ge(post_done, u + 1)
                    c0 = COLS["post_b"] + mt
                    act.activation(post[:, mt, cols_of(half)], acc_at(mt), ACT.Identity,
                                   bias=par[:, c0:c0 + 1]).then_inc(post_out, 1)
                    act.wait_ge(post_out, u + 1)
                    if half:
                        act.wait_ge(post_sums, 1)
                    act.activation(post_sq[:, mt], post[:, mt, cols_of(half)], ACT.Square).then_inc(post_sq_done, 1)
                if half == 0:
                    split_w(3, 1)
                    act.wait_ge(post_done, DC)
            act.wait_ge(post_done, 2 * DC)
            split_w(4, 0, 2 * DC * P)
            for half in range(2):
                act.wait_ge(p_eps, half + 1)
                act.activation(mr_st[half][:, HALF:], mr_st[half][:, HALF:], ACT.Sqrt).then_inc(p_root, 1)
                for mt in range(DC):
                    u = half * DC + mt
                    act.wait_ge(p_normed, u + 1)
                    g0, b0 = COLS["post_g"] + mt, COLS["post_be"] + mt
                    act.activation(post[:, mt, cols_of(half)], post[:, mt, cols_of(half)], ACT.Gelu,
                                   bias=par[:, b0:b0 + 1], scale=par[:, g0:g0 + 1]).then_inc(z_gelu, 1)
                    act.wait_ge(z_gelu, u + 1)
                    act.activation(act_hi[:, mt, cols_of(half)], post[:, mt, cols_of(half)],
                                   ACT.Copy).then_inc(z_hi_done, 1)
            for half in range(2):
                for mt in range(DC):
                    u = half * DC + mt
                    act.wait_ge(x_done, u + 1)
                    act.activation(act_hi[:, DC + mt, cols_of(half)], x_t[u % 2], ACT.Relu).then_inc(h1_hi_done, 1)
            act.wait_ge(z_lo_done, 2 * DC)
            for half in range(2):
                for mt in range(2):
                    act.wait_ge(top2_done, 2 * half + mt + 1)
                    c0 = COLS["b_top2"] + mt
                    act.activation(post[:, mt, cols_of(half)], ps[half][:, mt * 512:(mt + 1) * 512], ACT.Relu,
                                   bias=par[:, c0:c0 + 1]).then_inc(h2_done, 1)
            for half in range(2):
                act.wait_ge(y_done, half + 1)
                act.activation(post[0:1, 2, cols_of(half)], acc_at(half)[0:1, :], ACT.Copy).then_inc(y_out, 1)
            act.wait_ge(y_out, 2)
            act.dma_start(y, post[0:1, 2, :]).then_inc(y_stored, 16)
            act.wait_ge(y_stored, 16)

        @block.vector
        def _(dve):
            dve.memset(misc[1], 0.0).then_inc(zeroed, 1)
            dve.memset(ones[:, :], 1.0).then_inc(ones_done, 1)

            def split(g1, e, n=BLK):
                dve.wait_ge(w_hi_done, g1)
                dve.tensor_tensor(w_lo[:, e, 0:n], w_raw[:, 0:n], w_hi[:, e, 0:n].bitcast(F32),
                                  ALU.subtract).then_inc(w_lo_done, 1)

            def low(k, c):
                q = KC * k + c
                dve.wait_ge(act_hi_done, q + 1)
                dve.tensor_tensor(act_lo[:, c, :], ring[q % 3], act_hi[:, c, :].bitcast(F32),
                                  ALU.subtract).then_inc(act_lo_done, 1)

            def chunks(k):
                name = SETS[k]
                if name[0] != "h":
                    for c in range(KC):
                        low(k, c)
                    return
                norm = misc[1] if name == "h_r" else st
                if name == "h_r":
                    dve.wait_ge(st_back, 16)
                for c in range(KC):
                    q = KC * k + c
                    dve.wait_ge(raw_in[q % 3], 16 * (q // 3 + 1))
                    dve.tensor_tensor(ring[q % 3], ring[q % 3], norm[:, 0:B], ALU.subtract).then_inc(cent, 1)
                    dve.wait_ge(cent, KC * (k - 1) + c + 1)
                    dve.tensor_tensor(ring[q % 3], ring[q % 3], norm[:, B:2 * B], ALU.mult).then_inc(normed, 1)
                    if c:
                        low(k, c - 1)
                low(k, KC - 1)

            def statistics(s):
                dve.wait_ge(sums_done, s + 1)
                if s == 1:
                    dve.wait_ge(st_saved, 16)
                dve.tensor_scalar(st[:, 0:B], ps_st[0][:, :], 1.0 / HID, None, ALU.mult).then_inc(st_mean, 1)
                dve.wait_ge(st_mean, s + 1)
                dve.tensor_tensor(st[:, B:2 * B], st[:, 0:B], st[:, 0:B], ALU.mult).then_inc(st_msq, 1)
                dve.wait_ge(st_msq, s + 1)
                dve.scalar_tensor_tensor(out=st[:, B:2 * B], in0=ps_st[1][:, :], scalar=1.0 / HID,
                                         in1=st[:, B:2 * B], op0=ALU.mult, op1=ALU.subtract).then_inc(st_var, 1)
                dve.wait_ge(st_var, s + 1)
                dve.tensor_scalar(st[:, B:2 * B], st[:, B:2 * B], 0.0, 1e-5, ALU.max, ALU.add).then_inc(st_eps, 1)
                if s == 0:
                    dve.memset(misc[1], 0.0).then_inc(zeroed, 1)
                    dve.wait_ge(zeroed, 2)
                dve.wait_ge(st_root, s + 1)
                dve.reciprocal(st[:, B:2 * B], st[:, B:2 * B]).then_inc(st_recip, 1)

            split(1, 0)
            chunks(0)
            dve.wait_ge(zeroed, 1)
            for stage in STAGES:
                name, g0, n = stage

                def step(j, p):
                    if is_block(j, p, G_END - 1):
                        split(G_END + 1, 0, BLK // 2)
                    else:
                        split(2 * j + (p + 2), 1 - p)
                    if name in NEXT_SET and is_block(j, p, g0 + n - 1):
                        chunks(NEXT_SET[name])
                    if is_block(j, p, KC) or is_block(j, p, G_TOP):
                        statistics(1 * (g0 == G_TOP))
                    if name in ("l1_r", "l1_i"):
                        dve.wait_ge(evac, 2 * j + (p + 1))
                        if not is_block(j, p, 0):
                            dve.wait_ge(acc_done, 2 * j + p)
                        dve.tensor_tensor(acc, acc, hout[p], ALU.add).then_inc(acc_done, 1)

                blocks(dve, stage, step)
            for si in range(2):
                def matrix(m, last):
                    split(2 * m + (G_END + 6 * si + 2), 1, BLK // 2)
                    if not last:
                        split(2 * m + (G_END + 6 * si + 3), 0, BLK // 2)
                    elif si == 0:
                        split(G_END + 7, 0, BLK // 2)
                        chunks(4)

                matrix(0, False)
                matrix(1, False)
                matrix(2, True)
            for s in range(2):
                split(G_WO + s + 1, s)
            for half in range(2):
                dve.wait_ge(q_stored[half], 16 * 3 * DC * 2)
            dve.wait_ge(masks, 7)

            def split_wi(b, at=None):
                dve.wait_ge(wi_hi_done, b + 1)
                at = b + DC if at is None else at
                dve.tensor_tensor(act_lo[:, at, :], wi_raw, act_hi[:, at, :].bitcast(F32),
                                  ALU.subtract).then_inc(wi_lo_done, 1)

            def step(t, g):
                start, end = isinstance(t, int) and t == 0, isinstance(t, int) and t == TILES_B
                k1 = 4 * t + (g - 1)
                G1 = 4 * t + (g + 1)
                if not (start and g < 2):
                    for e in range(2):
                        dve.wait_ge(zT_done, 2 * k1 + (e - 1))
                        if not (start and g == 2):
                            dve.wait_ge(pv_done, 2 * k1 - 2)
                        dve.tensor_copy(wT[:, 4 * e:4 * e + 4, :],
                                        ps_st[0][:, e * 512:(e + 1) * 512].rearrange("p (h x) -> p h x", x=P))\
                           .then_inc(wT_done, 1)
                if not end:
                    for hh in range(2):
                        U1 = 8 * t + (2 * g + hh + 1)
                        dve.wait_ge(diag_done, 32 * t + (8 * g + 4 * hh + 4))
                        dve.tensor_tensor(sc[hh], sc[hh], same_row32[:, None, :].to_broadcast([P, 8, 32]),
                                          ALU.mult).then_inc(masked, 1)
                        dve.wait_ge(masked, U1)
                        dve.tensor_reduce(ar[:, 32 * hh:32 * hh + 32].rearrange("p (a m) -> p a m", m=N),
                                          sc[hh].rearrange("p a (b m) -> p a m b", m=N), AX.X, ALU.add)\
                           .then_inc(ar_done, 1)
                    dve.wait_ge(ar_done, 8 * t + (2 * g + 2))
                    dve.tensor_tensor(ar_sq, ar, ar, ALU.mult).then_inc(ar_sq_done, 1)
                    dve.wait_ge(ar_sq_done, G1)
                    sq4 = ar_sq.rearrange("p (h e m) -> p h e m", e=2, m=N)
                    dve.scalar_tensor_tensor(out=mag, in0=sq4[:, :, 0], scalar=1e-8, in1=sq4[:, :, 1],
                                             op0=ALU.add, op1=ALU.add).then_inc(mag2_done, 1)
                if not (start and g < 2):
                    for si in range(2):
                        dve.wait_ge(o_hi_done, 2 * k1 + (si - 1))
                        cs = slice((g + 2) % 4 * P, ((g + 2) % 4 + 1) * P)
                        oc = slice(si * HALF + cs.start, si * HALF + cs.stop)
                        dve.tensor_tensor(act_lo[:, 0:DC, oc],
                                          ps_st[1][:, si * 512:(si + 1) * 512].rearrange("p (c x) -> p c x", c=DC),
                                          act_hi[:, 0:DC, oc].bitcast(F32),
                                          ALU.subtract).then_inc(o_lo_done, 1)
                if not end:
                    dve.wait_ge(mag_done, G1)
                    dve.tensor_reduce(top, mag, AX.X, ALU.max).then_inc(top_done, 1)
                    dve.wait_ge(top_done, G1)
                    dve.tensor_tensor(ex, mag, top[:, :, None].to_broadcast([P, H, N]),
                                      ALU.subtract).then_inc(diff_done, 1)
                    dve.wait_ge(exp_done, G1)
                    dve.tensor_reduce(total, ex, AX.X, ALU.add).then_inc(total_done, 1)
                    dve.wait_ge(total_done, G1)
                    dve.reciprocal(inv, total).then_inc(inv_done, 1)
                    dve.wait_ge(inv_done, G1)
                    dve.tensor_tensor(wgt, ex, inv[:, :, None].to_broadcast([P, H, N]),
                                      ALU.mult).then_inc(wgt_done, 1)
                    dve.wait_ge(wgt_done, G1)
                    if not (start and g < 2):
                        dve.wait_ge(zT_done, 2 * k1)
                    for e in range(2):
                        hs = slice(4 * e, 4 * e + 4)
                        mm = dve.tensor_tensor(
                            z_w[g % 2][:, hs].rearrange("p h (b m) -> p h b m", m=N),
                            same_row[:, None, :].to_broadcast([P, 4, P]).rearrange("p h (b m) -> p h b m", m=N),
                            wgt[:, hs, None, :].to_broadcast([P, 4, 32, N]), ALU.mult)
                        mm.then_inc(z_done, 1)
                if start and g > 0:
                    for b in WI_FIRST[g]:
                        split_wi(b)
                if not isinstance(t, int) and g == 1:
                    split_wi(t + (WI_LOOP - 1))

            groups(dve, step)

            for b in range(12, 16):
                split_wi(b, b - 12)

            def split_a(t, pos):
                e = pos % 2
                dve.wait_ge(a_hi_done, 8 * t + 2 * (pos + 1))
                dve.tensor_tensor(w_lo[:, e, 0:1024], a_raw.rearrange("p s c x -> p (s c x)"),
                                  w_hi[:, e, 0:1024].bitcast(F32), ALU.subtract).then_inc(a_lo_done, 1)

            def quarter(t, q, between=None):
                Q1 = 4 * t + (q + 1)
                C = rt[q % 2]

                def s_(i, j):
                    return strength[:, bass.ds(t, 1), N * i + j]

                dve.wait_ge(rinv_done, Q1)
                dve.tensor_tensor(un[:, 0], z[:, q, 0], C, ALU.mult).then_inc(ur_done, 1)
                dve.wait_ge(ur_done, Q1)
                for d in range(1, N):
                    mm = dve.tensor_tensor(t_r[:, AT[d][0]:AT[d][1]], un[:, 0, 0:N - d], un[:, 0, d:N], ALU.mult)
                mm.then_inc(tr_done, 1)
                dve.wait_ge(tr_done, Q1)
                dve.wait_ge(zero_marked, Q1)
                if q == 0:
                    for d in range(1, N):
                        part = t_r[:, AT[d][0]:AT[d][1]]
                        mm = dve.tensor_tensor(part, part, m2[0][:, 0:N - d], ALU.add)
                    mm.then_inc(t_first, 1)
                    dve.wait_ge(t_first, t + 1)
                for d in range(1, N):
                    part = t_r[:, AT[d][0]:AT[d][1]]
                    mm = dve.tensor_tensor(part, part, m2[q % 2][:, d:N], ALU.add)
                mm.then_inc(t_marked, 1)
                dve.wait_ge(t_marked, Q1)
                dve.wait_ge(ti_done, Q1)
                dve.tensor_tensor(t_r, t_r, t_i, ALU.add).then_inc(t_done, 1)
                dve.wait_ge(t_done, Q1)
                if between:
                    between()
                for k in range(3):
                    if k:
                        dve.wait_ge(c_round, 12 * t + (3 * q + k))
                    for j in range(N):
                        i = [i for i in range(N) if i != j][k]
                        pair = t_r[:, PAIRS.index((min(i, j), max(i, j)))]
                        if k == 0:
                            mm = dve.tensor_scalar(C[:, j], pair, s_(i, j), s_(j, j), ALU.mult, ALU.add)
                        else:
                            mm = dve.scalar_tensor_tensor(out=C[:, j], in0=pair, scalar=s_(i, j), in1=C[:, j],
                                                          op0=ALU.mult, op1=ALU.add)
                    mm.then_inc(c_round, 1)
                dve.wait_ge(c_round, 12 * t + 3 * (q + 1))
                zq = z[:, q]
                dve.tensor_tensor(zq, zq, C[:, None].to_broadcast([P, 2, N, P]), ALU.mult).then_inc(prod_done, 1)
                dve.wait_ge(prod_done, Q1)
                dve.tensor_tensor(zq[:, :, 0:2], zq[:, :, 0:2], zq[:, :, 2:4], ALU.add).then_inc(half_sum, 1)
                dve.wait_ge(half_sum, Q1)

            def sum_up(t, q):
                if q == 0 and not (isinstance(t, int) and t == 0):
                    dve.wait_ge(sup_stored, 32 * t)
                dve.tensor_tensor(sup[:, :, q * P:(q + 1) * P], z[:, q, :, 0], z[:, q, :, 1],
                                  ALU.add).then_inc(sup_done, 1)

            def norm(t1):
                dve.wait_ge(nrm_inv, t1)
                dve.tensor_scalar(sup, sup, nrm[:, 1:2], None, ALU.mult).then_inc(scaled, 1)

            for t, pos in [(0, 0), (0, 1), (0, 2), (0, 3), (1, 0)]:
                split_a(t, pos)
            dve.wait_ge(strength_in, 16 * TILES_B * N)

            def step(t):
                last = isinstance(t, int) and t == TILES_B - 1

                def between():
                    if not (isinstance(t, int) and t == 0):
                        norm(t)
                    if not last:
                        split_a(t + 1, 1)

                quarter(t, 0, between)
                quarter(t, 1, None if last else lambda: split_a(t + 1, 2))
                for q in range(2):
                    sum_up(t, q)
                quarter(t, 2, None if last else lambda: split_a(t + 1, 3))
                sum_up(t, 2)
                quarter(t, 3, None if isinstance(t, int) and t >= TILES_B - 2 else lambda: split_a(t + 2, 0))
                sum_up(t, 3)

            tiles(dve, step)
            norm(TILES_B)

            split(G_WO + 3, 0)
            split(G_WO + 4, 1)
            for c in range(2 * DC):
                q = 5 * KC + c
                dve.wait_ge(act_hi_done, q + 1)
                if c >= DC:
                    dve.tensor_tensor(act_lo[:, c + DC, :], act_hi[:, c, :].bitcast(F32), ring[q % 3], ALU.subtract)
                dve.tensor_tensor(act_lo[:, c, :], ring[q % 3], act_hi[:, c, :].bitcast(F32),
                                  ALU.subtract).then_inc(act_lo_done, 1)
            for u in range(2 * DC):
                half, mt = u // DC, u % DC
                dve.wait_ge(m_sq_done, u + 1)
                dve.tensor_tensor(x_t[u % 2], m_sq[:, 0:HALF], m_sq[:, HALF:], ALU.add).then_inc(amp2_done, 1)
                dve.wait_ge(amp_hi_done, u + 1)
                dve.tensor_tensor(act_lo[:, 3 * DC + mt, cols_of(half)], x_t[u % 2],
                                  act_hi[:, 3 * DC + mt, cols_of(half)].bitcast(F32),
                                  ALU.subtract).then_inc(amp_lo_done, 1)
            split(G_WO + 5, 0)
            split(G_WO + 6, 1)
            for half in range(2):
                M, S = mr_st[half][:, 0:HALF], mr_st[half][:, HALF:]
                dve.wait_ge(post_sums, half + 1)
                if half == 1:
                    split(G_WO + 7, 0, 2 * DC * P)
                dve.tensor_scalar(M, ps[half][:, 0:HALF], 1.0 / OUT, None, ALU.mult).then_inc(p_mean, 1)
                dve.wait_ge(p_mean, half + 1)
                dve.tensor_tensor(S, M, M, ALU.mult).then_inc(p_msq, 1)
                dve.wait_ge(p_msq, half + 1)
                dve.scalar_tensor_tensor(out=S, in0=ps[half][:, HALF:], scalar=1.0 / OUT, in1=S, op0=ALU.mult,
                                         op1=ALU.subtract).then_inc(p_var, 1)
                dve.wait_ge(p_var, half + 1)
                dve.tensor_scalar(S, S, 0.0, 1e-5, ALU.max, ALU.add).then_inc(p_eps, 1)
                dve.wait_ge(p_root, half + 1)
                dve.reciprocal(S, S).then_inc(p_inv, 1)
                dve.wait_ge(p_inv, half + 1)
                for mt in range(DC):
                    x = post[:, mt, cols_of(half)]
                    dve.tensor_tensor(x, x, M, ALU.subtract).then_inc(p_cent, 1)
                    dve.wait_ge(p_cent, half * DC + mt + 1)
                    dve.tensor_tensor(x, x, S, ALU.mult).then_inc(p_normed, 1)
                for mt in range(DC):
                    u = half * DC + mt
                    dve.wait_ge(z_hi_done, u + 1)
                    dve.tensor_tensor(act_lo[:, mt, cols_of(half)], post[:, mt, cols_of(half)],
                                      act_hi[:, mt, cols_of(half)].bitcast(F32), ALU.subtract).then_inc(z_lo_done, 1)
            for u in range(2 * DC):
                half, mt = u // DC, u % DC
                dve.wait_ge(top1_done, u + 1)
                dve.wait_ge(top_in[u % 2], 16 * (u // 2 + 1))
                if u == 0:
                    dve.wait_ge(post_sums, 2)
                dve.tensor_tensor(x_t[u % 2], acc_at(mt), top_x[u % 2], ALU.add).then_inc(x_done, 1)
                dve.wait_ge(h1_hi_done, u + 1)
                dve.scalar_tensor_tensor(out=act_lo[:, DC + mt, cols_of(half)], in0=x_t[u % 2], scalar=0.0,
                                         in1=act_hi[:, DC + mt, cols_of(half)].bitcast(F32), op0=ALU.max,
                                         op1=ALU.subtract).then_inc(h1_lo_done, 1)

        @block.gpsimd
        def _(pool):
            pool.memset(ident[:, :], 0.0).then_inc(ident_z, 1)
            pool.memset(zero[:, :], 0.0).then_inc(ident_z, 1)
            pool.memset(tiny[:, 0:1], 1e-37).then_inc(ident_z, 1)
            pool.memset(tiny[:, 1:2], 1e-8).then_inc(ident_z, 1)
            pool.memset(same_row[:, :], 1.0).then_inc(ident_z, 1)
            pool.wait_ge(ident_z, 5)
            pool.affine_select(out=ident[:, :], in_=ident[:, :], compare_op=ALU.not_equal, fill=1.0, base=0,
                               pattern=[[-1, P]], channel_multiplier=1).then_inc(masks, 1)
            pool.affine_select(out=same_row[:, :], in_=same_row[:, :], compare_op=ALU.is_ge, fill=0.0, base=0,
                               pattern=[[-N, P // N], [0, N]], channel_multiplier=1).then_inc(masks, 1)
            pool.wait_ge(masks, 2)
            pool.affine_select(out=same_row[:, :], in_=same_row[:, :], compare_op=ALU.is_ge, fill=0.0, base=N - 1,
                               pattern=[[N, P // N], [0, N]], channel_multiplier=-1).then_inc(masks, 1)
            pool.wait_ge(masks, 3)
            for qd in range(4):
                rows = slice(32 * qd, 32 * qd + 32)
                pool.tensor_copy(same_row32[rows, :], same_row[rows, rows]).then_inc(masks, 1)
            pool.wait_ge(masks, 7)
            pool.dma_start(ids_sb[:, :, :], ids.rearrange("(t p) n -> p t n", p=P)).then_inc(ids_in, 16)
            pool.wait_ge(ids_in, 16)
            for t in range(TILES_B):
                for i in range(N):
                    pool.indirect_dma_start(strength[:, t, N * i:N * (i + 1)], None, tbl[i],
                                            bass.IndirectOffsetOnAxis(ids_sb[:, t, i:i + 1], 0))\
                        .then_inc(strength_in, 16)
            pool.wait_ge(zeroed, 1)
            for stage in STAGES:
                name, g0, n = stage

                def step(j, p):
                    pool.wait_ge(evac, 2 * j + (p + 1))
                    pool.dma_start(OUTS[name][2 * j + (p - g0)], hout[p]).then_inc(stored[p], 16)
                    if name in ("l1_r", "l1_i"):
                        if is_block(j, p, KC):
                            pool.wait_ge(zeroed, 2)
                        if not is_block(j, p, 0):
                            pool.wait_ge(acc2_done, 2 * j + p)
                        pool.tensor_tensor(sq, hout[p], hout[p], ALU.mult).then_inc(sq_done, 1)
                        pool.wait_ge(sq_done, 2 * j + (p + 1))
                        pool.tensor_tensor(acc2, acc2, sq, ALU.add).then_inc(acc2_done, 1)
                    if is_block(j, p, KC):
                        pool.wait_ge(st_recip, 1)
                        pool.dma_start(stat_rows, st[0:1, :]).then_inc(st_saved, 16)

                blocks(pool, stage, step)
            for si, s in enumerate("ri"):
                with pool.Fori(0, 3) as m:
                    for mt in range(DC):
                        for half in range(2):
                            v = 2 * mt + half
                            pool.wait_ge(tile_evac, 2 * N * DC * m + (TILES_Q * si + N * (v + 1)))
                            pool.dma_start(qkvT[s][m, mt * P:(mt + 1) * P, half * 2048:(half + 1) * 2048],
                                           misc[half]).then_inc(q_stored[half], 16)

            def step(t, g):
                if not (isinstance(t, int) and t == TILES_B):
                    for hh in range(2):
                        pool.wait_ge(qk_in[hh], 384 * t + 96 * (g + 1))
                        pool.tensor_tensor(kk_u[hh][0:64, :, 1], zero[0:64, :, None].to_broadcast([64, HU, P]),
                                           kk_u[hh][0:64, :, 1], ALU.subtract).then_inc(negated, 1)

            groups(pool, step)

            def add_squares(t, q):
                pool.wait_ge(z_sq_done, 4 * t + (q + 1))
                pool.tensor_tensor(m2[q % 2], z_sq[q % 2][:, 0], z_sq[q % 2][:, 1], ALU.add).then_inc(m2_done, 1)

            def split_negated(t, pos):
                pool.wait_ge(a_hi_done, 8 * t + 2 * (pos + 1))
                pool.tensor_tensor(w_lo[:, pos % 2, 1024:1536], w_hi[:, pos % 2, 512:1024].bitcast(F32),
                                   a_raw[:, 1].rearrange("p c x -> p (c x)"), ALU.subtract).then_inc(neg_lo_done, 1)

            for t, pos in [(0, 0), (0, 1), (0, 2), (0, 3), (1, 0)]:
                split_negated(t, pos)

            def step(t):
                add_squares(t, 0)
                for q in range(4):
                    Q1 = 4 * t + (q + 1)
                    pool.wait_ge(rinv_done, Q1)
                    pool.tensor_tensor(un[:, 1], z[:, q, 1], rt[q % 2], ALU.mult).then_inc(ui_done, 1)
                    pool.tensor_scalar(m2[q % 2], m2[q % 2], 0.0, None, ALU.is_equal).then_inc(zero_marked, 1)
                    if q in (1, 2):
                        add_squares(t, q + 1)
                    pool.wait_ge(ui_done, Q1)
                    if not (isinstance(t, int) and t == 0 and q == 0):
                        pool.wait_ge(t_done, Q1 - 1)
                    for d in range(1, N):
                        mm = pool.tensor_tensor(t_i[:, AT[d][0]:AT[d][1]], un[:, 1, 0:N - d], un[:, 1, d:N],
                                                ALU.mult)
                    if q:
                        mm.then_inc(t_mult, 1)
                        pool.wait_ge(zero_marked, Q1)
                        pool.wait_ge(t_mult, 3 * t + q)
                        for d in range(1, N):
                            part = t_i[:, AT[d][0]:AT[d][1]]
                            mm = pool.tensor_tensor(part, part, m2[q % 2][:, 0:N - d], ALU.add)
                    mm.then_inc(ti_done, 1)
                    if q == 0:
                        add_squares(t, 1)
                    if q < 3 and not (isinstance(t, int) and t == TILES_B - 1):
                        split_negated(t + 1, q + 1)
                if not (isinstance(t, int) and t >= TILES_B - 2):
                    split_negated(t + 2, 0)

            tiles(pool, step)

        @block.tensor
        def _(pe):
            def three(out, lhs_hi, lhs_lo, rhs_hi, rhs_lo, start, stop):
                pe.matmul(out, lhs_hi, rhs_hi, start=start, stop=False)
                pe.matmul(out, lhs_hi, rhs_lo, start=False, stop=False)
                return pe.matmul(out, lhs_lo, rhs_hi, start=False, stop=stop)

            def wide(j, p, k=None):
                pe.wait_ge(w_lo_done, 2 * j + (p + 1))
                if not (isinstance(j, int) and j == 0):
                    pe.wait_ge(evac, 2 * j + p - 1)
                for c in range(KC):
                    if k is not None:
                        pe.wait_ge(act_lo_done, KC * k + c + 1)
                    for half in range(2):
                        cs = slice(half * HALF, (half + 1) * HALF)
                        mm = three(ps[p][:, cs], w_hi[:, p, c * P:(c + 1) * P], w_lo[:, p, c * P:(c + 1) * P],
                                   act_hi[:, c, cs], act_lo[:, c, cs], c == 0, c == KC - 1)
                    mm.then_inc(used, 1)

            def sums(s):
                pe.wait_ge(acc_done, KC * (s + 1))
                pe.wait_ge(acc2_done, KC * (s + 1))
                pe.wait_ge(ones_done, 1)
                if s == 1:
                    pe.wait_ge(st_var, 1)
                for half in range(2):
                    cs = slice(half * HALF, (half + 1) * HALF)
                    pe.matmul(ps_st[0][:, cs], ones[:, :], acc[:, cs], start=True, stop=True)
                    mm = pe.matmul(ps_st[1][:, cs], ones[:, :], acc2[:, cs], start=True, stop=True)
                mm.then_inc(sums_done, 1)

            FIRST = {"l1_r": 0, "l2_r": 1, "l2_i": 2}
            for stage in STAGES:
                name, g0, n = stage

                def step(j, p):
                    wide(j, p, FIRST[name] if name in FIRST and is_block(j, p, g0) else None)
                    if is_block(j, p, KC) or is_block(j, p, G_TOP):
                        sums(1 * (g0 == G_TOP))

                blocks(pe, stage, step)

            for si, s in enumerate("ri"):
                T0 = TILES_Q * si

                def matrix(m, first):
                    for e in range(2):
                        pe.wait_ge(w_lo_done, 2 * m + (G_END + 6 * si + e + 1))
                        for mt in range(2 * e, 2 * e + 2):
                            for half in range(2):
                                cs = slice(half * HALF, (half + 1) * HALF)
                                for n in range(N):
                                    i = (mt * 2 + half) * N + n
                                    if not (first and si == 0 and i < 4):
                                        pe.wait_ge(tile_evac, 2 * N * DC * m + (T0 + i - 3))
                                    for kc in range(DC):
                                        c = n * DC + kc
                                        if first and mt == 0 and half == 0:
                                            pe.wait_ge(act_lo_done, KC * (3 + si) + c + 1)
                                        ws = slice((mt % 2 * DC + kc) * P, (mt % 2 * DC + kc + 1) * P)
                                        mm = three(ps_st[i // 2 % 2][:, (i % 2) * HALF:(i % 2 + 1) * HALF],
                                                   w_hi[:, e, ws], w_lo[:, e, ws],
                                                   act_hi[:, c, cs], act_lo[:, c, cs], kc == 0, kc == DC - 1)
                                    mm.then_inc(tile_done, 1)

                matrix(0, True)
                with pe.Fori(1, 3) as m:
                    matrix(m, False)

            pe.wait_ge(evac, G_END)
            pe.wait_ge(tile_evac, 2 * TILES_Q)
            pe.wait_ge(masks, 1)

            def step(t, g):
                start, end = isinstance(t, int) and t == 0, isinstance(t, int) and t == TILES_B
                k1 = 4 * t + (g - 1)

                def scores(hh):
                    U1 = 8 * t + (2 * g + hh + 1)
                    pe.wait_ge(negated, U1)
                    if not (start and g == 0):
                        pe.wait_ge(diag_done, 32 * t + (8 * g + 4 * hh - 4))
                    for h in range(HU):
                        mm = pe.matmul(ps[hh][:, h * 256:(h + 1) * 256], q_u[hh][:, h, :],
                                       kk_u[hh][:, h].rearrange("p e x -> p (e x)"), start=True, stop=True)
                    mm.then_inc(scores_done, 1)

                if not (start and g < 2):
                    pe.wait_ge(v_in, 32 * k1)
                    if not (start and g == 2):
                        pe.wait_ge(wT_done, 2 * k1 - 2)
                    if not start:
                        pe.wait_ge(a_out_done, 8 * t if g > 1 else 8 * t - 8) if not (
                            isinstance(t, int) and t == 1 and g < 2) else None
                    for si in range(2):
                        for c in range(DC):
                            mm = pe.transpose(ps_st[0][:, si * 512 + c * P:si * 512 + (c + 1) * P],
                                              v_raw[:, si, c, :], ident[:, :])
                        mm.then_inc(vT_done, 1)
                if not end:
                    scores(0)
                if not (start and g < 2):
                    for e in range(2):
                        pe.wait_ge(z_done, 2 * k1 + (e - 1))
                        pe.wait_ge(v_nat_done, 2 * k1 + (e - 1))
                        for h in range(4):
                            mm = pe.transpose(ps_st[0][:, e * 512 + h * P:e * 512 + (h + 1) * P],
                                              z_w[g % 2][:, 4 * e + h, :], ident[:, :])
                        mm.then_inc(zT_done, 1)
                if not end:
                    scores(1)
                if not (start and g < 2):
                    if not (start and g == 2):
                        pe.wait_ge(o_lo_done, 2 * k1 - 2)
                    for si in range(2):
                        for h in range(H):
                            if si == 0 and h % 4 == 0:
                                pe.wait_ge(wT_done, 2 * k1 + (h // 4 - 1))
                            lo = 64 * (h % 2)
                            mm = pe.matmul(ps_st[1][lo:lo + 64, si * 512 + h // 2 * P:si * 512 + (h // 2 + 1) * P],
                                           v_nat[:, si, h * HD:(h + 1) * HD], wT[:, h, :], start=True, stop=True)
                        mm.then_inc(pv_done, 1)
                if g == 1 and not start:
                    if isinstance(t, int) and t == 1 or True:
                        pe.wait_ge(w_lo_done, G_WO + 2)
                    pe.wait_ge(o_lo_done, 8 * t)
                    for i in range(2 * DC):
                        si, mt = i // DC, i % DC
                        if i >= 2:
                            pe.wait_ge(a_out_done, 8 * t + (i - 9))
                        for kc in range(DC):
                            ws = slice((mt * DC + kc) * P, (mt * DC + kc + 1) * P)
                            mm = three(ps_st[0][:, (i % 2) * 512:(i % 2 + 1) * 512], w_hi[:, si, ws], w_lo[:, si, ws],
                                       act_hi[:, kc, si * HALF:(si + 1) * HALF],
                                       act_lo[:, kc, si * HALF:(si + 1) * HALF],
                                       kc == 0, kc == DC - 1)
                        mm.then_inc(wo_done, 1)

            groups(pe, step)

            acc_of = [ps[0], ps[1], ps_st[0], ps_st[1]]
            pe.wait_ge(diag_done, 4 * 2 * GROUPS)
            pe.wait_ge(a_out_done, 2 * DC * TILES_B)
            pe.wait_ge(o_lo_done, 2 * GROUPS)

            def interact(t, turn=False):
                start = isinstance(t, int) and t == 0
                for pos in range(N):
                    n, e = (pos + 1) % N, pos % 2
                    if start and pos in (0, N - 1):
                        pe.wait_ge(wi_lo_done, 16 if pos else 12)
                    if not start:
                        pe.wait_ge(z_out, 8 * t + (pos - 3))
                    if pos == 1 and turn:
                        turn_sup(t - 1)
                    if pos == N - 1 and turn:
                        pe.wait_ge(supT_out, 2 * t - 2)
                    pe.wait_ge(a_lo_done, 4 * t + (pos + 1))
                    pe.wait_ge(neg_lo_done, 4 * t + (pos + 1))
                    for im in range(2):
                        out = acc_of[pos][:, im * 512:(im + 1) * 512]
                        for kc in range(DC):
                            for si in range(2):
                                a0 = (si if im else 2 * si) * 512 + kc * P
                                wc, wo = DC * n + 2 * (si ^ im) + kc // 2, (kc % 2) * 512
                                mm = three(out, w_hi[:, e, a0:a0 + P], w_lo[:, e, a0:a0 + P],
                                           act_hi[:, wc, wo:wo + 512], act_lo[:, wc, wo:wo + 512],
                                           kc == 0 and si == 0, kc == DC - 1 and si == 1)
                    mm.then_inc(int_done, 1)

            def turn_sup(t1):
                pe.wait_ge(scaled, t1)
                if isinstance(t1, int) and t1 == TILES_B:
                    pe.wait_ge(supT_out, 2 * t1 - 2)
                else:
                    pe.wait_ge(z_out, 8 * t1 + 8)
                for e in range(2):
                    for c in range(DC):
                        mm = pe.transpose(ps_st[1][:, e * 512 + c * P:e * 512 + (c + 1) * P],
                                          sup[:, e, c * P:(c + 1) * P], ident[:, :])
                    mm.then_inc(supT_done, 1)

            interact(0)

            def step(t):
                if not (isinstance(t, int) and t == TILES_B - 1):
                    interact(t + 1, not (isinstance(t, int) and t == 0))
                else:
                    turn_sup(t)

            tiles(pe, step)
            turn_sup(TILES_B)

            pe.wait_ge(w_lo_done, G_WO + 4)
            pe.wait_ge(act_lo_done, 5 * KC + 2 * DC)
            pe.wait_ge(supT_out, 2 * TILES_B)
            for u in range(2 * DC):
                half, mt = u // DC, u % DC
                cs = cols_of(half)
                if u >= 2:
                    pe.wait_ge(m_sq_done, u - 1)
                for im in range(2):
                    for si in range(2):
                        for kc in range(DC):
                            ws = slice((mt * DC + kc) * P, (mt * DC + kc + 1) * P)
                            c = (si if im else 2 * si) * DC + kc
                            e = si ^ im
                            mm = three(ps[u % 2][:, im * 512:(im + 1) * 512], w_hi[:, e, ws], w_lo[:, e, ws],
                                       act_hi[:, c, cs], act_lo[:, c, cs],
                                       kc == 0 and si == 0, kc == DC - 1 and si == 1)
                mm.then_inc(meas_done, 1)

            def layer(out, e, mt, half, c0):
                for kc in range(DC):
                    ws = slice((mt * DC + kc) * P, (mt * DC + kc + 1) * P)
                    mm = three(out, w_hi[:, e, ws], w_lo[:, e, ws], act_hi[:, c0 + kc, cols_of(half)],
                               act_lo[:, c0 + kc, cols_of(half)], kc == 0, kc == DC - 1)
                return mm

            pe.wait_ge(w_lo_done, G_WO + 5)
            for half in range(2):
                pe.wait_ge(amp_lo_done, DC * (half + 1))
                for mt in range(DC):
                    if half:
                        pe.wait_ge(post_out, mt + 1)
                    layer(acc_at(mt), 0, mt, half, 3 * DC).then_inc(post_done, 1)
                pe.wait_ge(m_sq_done, 2 * DC)
                for mt in range(DC):
                    pe.wait_ge(post_out, DC * half + mt + 1)
                    pe.matmul(ps[half][:, 0:HALF], ones[:, :], post[:, mt, cols_of(half)],
                              start=(mt == 0), stop=(mt == DC - 1))
                for mt in range(DC):
                    pe.wait_ge(post_sq_done, DC * half + mt + 1)
                    mm = pe.matmul(ps[half][:, HALF:], ones[:, :], post_sq[:, mt],
                                   start=(mt == 0), stop=(mt == DC - 1))
                mm.then_inc(post_sums, 1)
            pe.wait_ge(w_lo_done, G_WO + 6)
            for half in range(2):
                pe.wait_ge(z_lo_done, DC * (half + 1))
                for mt in range(DC):
                    pe.wait_ge(x_done, mt + 1) if half else pe.wait_ge(post_out, 2 * DC)
                    layer(acc_at(mt), 1, mt, half, 0).then_inc(top1_done, 1)
            pe.wait_ge(w_lo_done, G_WO + 7)
            for half in range(2):
                pe.wait_ge(h1_lo_done, DC * (half + 1))
                for mt in range(2):
                    layer(ps[half][:, mt * 512:(mt + 1) * 512], 0, mt, half, DC).then_inc(top2_done, 1)
            pe.wait_ge(x_done, 2 * DC)
            for half in range(2):
                pe.wait_ge(h2_done, 2 * half + 2)
                for kc in range(2):
                    c0 = COLS["w_top3"] + kc
                    mm = pe.matmul(acc_at(half)[0:1, :], par[:, c0:c0 + 1], post[:, kc, cols_of(half)],
                                   start=(kc == 0), stop=(kc == 1))
                mm.then_inc(y_done, 1)


def block_layout(WT):
    K, M = WT.shape
    return WT.reshape(K // P, P, M // P, P).transpose(2, 1, 0, 3).reshape(M // P, P, K)


def kernel(**inputs):
    import numpy as np
    import concourse.bacc as bacc
    from concourse.bass_utils import run_bass_kernel_spmd

    a = {k: np.asarray(v) for k, v in inputs.items()}
    L = {k[7:]: v for k, v in a.items() if k.startswith("L0_rec_")}
    host = {"xT": a["r_x"].T.reshape(KC, P, B), "ids": a["ids"]}
    for i in range(4):
        host[f"tbl_{i}"] = a[f"tbl_{i}"]
    W = {"l1_r": block_layout(L["er_W1"].T), "l1_i": block_layout(L["ei_W1"].T),
         "l2_r": block_layout(L["er_W2"].T), "l2_i": block_layout(L["ei_W2"].T),
         "top1x": block_layout(a["W_top1"][OUT:])}
    for s in "ri":
        W["qkv_" + s] = np.stack([block_layout(L[f"W{m}_{s}"].T).transpose(1, 0, 2).reshape(P, BLK)
                                  for m in "qkv"])
    W["o"] = np.stack([block_layout(L["Wo_" + s].T).transpose(1, 0, 2).reshape(P, BLK) for s in "ri"])
    pieces = np.stack([L["int_Wr"], L["int_Wi"]], axis=1).transpose(0, 1, 3, 2)
    pieces = pieces.reshape(N, 2, 2, 2, P, D).transpose(0, 1, 2, 4, 3, 5).reshape(N, 4, P, 2 * D)
    W["int"] = pieces[[1, 2, 3, 0]].reshape(4 * N, P, 2 * D)
    W["meas"] = np.stack([block_layout(L["meas_M" + s].T).transpose(1, 0, 2).reshape(P, BLK) for s in "ri"])
    W["post"] = block_layout(L["post_W"].T).transpose(1, 0, 2).reshape(P, BLK)
    W["top1z"] = block_layout(a["W_top1"][:OUT]).transpose(1, 0, 2).reshape(P, BLK)
    W["top2"] = block_layout(a["W_top2"]).transpose(1, 0, 2).reshape(P, 2 * DC * P)
    for k, v in W.items():
        host["w_" + k] = v

    def col(v):
        return v.reshape(-1, P).T

    parts = {"b1_r": L["er_b1"], "b1_i": L["ei_b1"], "b_top1": a["b_top1"], "b2_r": L["er_b2"],
             "b2_i": L["ei_b2"], "g_r": L["er_g1"], "be_r": L["er_be1"], "g_i": L["ei_g1"], "be_i": L["ei_be1"],
             "bqkv_r": np.concatenate([L["bq_r"], L["bk_r"], L["bv_r"]]),
             "bqkv_i": np.concatenate([L["bq_i"], L["bk_i"], L["bv_i"]]),
             "bo_r": L["bo_r"], "bo_i": L["bo_i"], "post_b": L["post_b"], "post_g": L["post_g"],
             "post_be": L["post_be"], "b_top2": a["b_top2"], "w_top3": a["W_top3"]}
    host["cols"] = np.concatenate([col(parts[k]) for k in COLS], axis=1)
    host = {k: np.ascontiguousarray(v) for k, v in host.items()}

    nc = bacc.Bacc("TRN2", target_bir_lowering=False, num_devices=1)
    t = {k: nc.dram_tensor("in_" + k, list(v.shape), mybir.dt.from_np(v.dtype), kind="ExternalInput").ap()
         for k, v in host.items()}
    y = nc.dram_tensor("y", [1, B], F32, kind="ExternalOutput").ap()
    build(nc, t["xT"], t["ids"], [t[f"tbl_{i}"] for i in range(4)],
          {k[2:]: v for k, v in t.items() if k[:2] == "w_"}, t["cols"], y)
    r = run_bass_kernel_spmd(nc, [{"in_" + k: v for k, v in host.items()}], core_ids=[0])
    return np.asarray(r.results[0]["y"]).reshape(B, 1)
```

```python
from contextlib import ExitStack

import concourse.bass as bass
from concourse import mybir

F32 = mybir.dt.float32
F32R = mybir.dt.float32r
I32 = mybir.dt.int32
ACT = mybir.ActivationFunctionType
ALU = mybir.AluOpType
AX = mybir.AxisListType

P = 128
LN_EXP_SET = 6
SCRATCH = "Internal"
B, IN, HID, D, N, OUT = 1024, 2048, 2048, 512, 4, 512
H = 8
HD = D // H
KC = IN // P
DC = D // P
HALF = B // 2
BLK = KC * P

COLS = {}
_at = 0
for _name, _n in (("b1_r", KC), ("b1_i", KC), ("b_top1", DC), ("b2_r", KC), ("b2_i", KC),
                  ("g_r", KC), ("be_r", KC), ("g_i", KC), ("be_i", KC),
                  ("bqkv_r", 3 * DC), ("bqkv_i", 3 * DC), ("bo_r", DC), ("bo_i", DC),
                  ("post_b", DC), ("post_g", DC), ("post_be", DC), ("b_top2", 2), ("w_top3", 2)):
    COLS[_name] = _at
    _at += _n
NCOLS = _at

G_L1 = {"r": 0, "i": KC}
G_TOP = 2 * KC
G_L2 = {"r": G_TOP + DC, "i": G_TOP + DC + KC}
G_END = G_L2["i"] + KC
G_WO = G_END + 6 * 2
GROUPS = B * N // P
TILES_B = B // P
HU = H // 2
TILES_Q = 3 * DC * 2 * N


def build(nc, xT, ids, tbl, w, cols, y):
    hT = {s: nc.dram_tensor(f"hT_{s}", [KC, P, B], F32, kind=SCRATCH).ap() for s in "ri"}
    sT = {s: nc.dram_tensor(f"sT_{s}", [KC, P, B], F32, kind=SCRATCH).ap() for s in "ri"}
    topT = nc.dram_tensor("topT", [DC, P, B], F32, kind=SCRATCH).ap()
    stat_rows = nc.dram_tensor("stat_rows", [1, 2 * B], F32, kind=SCRATCH).ap()
    qkT = {s: nc.dram_tensor(f"qkT_{s}", [2, 2, D // 2, B * N], F32, kind=SCRATCH).ap() for s in "ri"}
    valT = {s: nc.dram_tensor(f"valT_{s}", [D, B * N], F32, kind=SCRATCH).ap() for s in "ri"}

    attnT = {s: nc.dram_tensor(f"attnT_{s}", [DC, P, N, B], F32, kind=SCRATCH).ap() for s in "ri"}

    supT = nc.dram_tensor("supT", [2, DC, P, B], F32, kind=SCRATCH).ap()

    ctx = ExitStack()
    with ctx:
        def sb(name, shape, dt=F32):
            return ctx.enter_context(nc.sbuf_tensor(name, shape, dt))

        def sem(name):
            return ctx.enter_context(nc.semaphore(name))

        act_hi = sb("act_hi", [P, KC, B], F32R)
        act_lo = sb("act_lo", [P, KC, B], F32R)
        w_hi = sb("w_hi", [P, 2, BLK], F32R)
        w_lo = sb("w_lo", [P, 2, BLK], F32R)
        arena = sb("arena", [P, 11264])
        par = sb("par", [P, NCOLS])
        ones = sb("ones", [P, P])

        w_raw = arena[:, 0:BLK]
        ring = [arena[:, 2048 + 1024 * i:2048 + 1024 * (i + 1)] for i in range(3)]
        misc = [arena[:, 5120 + 2048 * i:5120 + 2048 * (i + 1)] for i in range(3)]
        hout = [misc[0][:, 0:B], misc[0][:, B:2 * B]]
        acc, acc2 = misc[1][:, 0:B], misc[1][:, B:2 * B]
        st = misc[2]
        sq = ring[2]
        qout = [m.rearrange("p (b n) -> p b n", n=N) for m in misc[:2]]

        ps = [ctx.enter_context(nc.psum_tensor(f"ps{i}", [P, B], F32)) for i in range(2)]
        ps_st = [ctx.enter_context(nc.psum_tensor(f"ps_st{i}", [P, B], F32)) for i in range(2)]

        zero = sb("zero", [P, 1])
        ident = sb("ident", [P, P])
        same_row = sb("same_row", [P, P])
        same_row32 = sb("same_row32", [P, 32])
        v_raw = arena[:, 0:1024].rearrange("p (s c x) -> p s c x", s=2, c=DC)
        wi_raw = arena[:, 1024:2048]
        qk = [arena[:, 2048 + 1536 * i:2048 + 1536 * (i + 1)] for i in range(2)]
        qkk = [x.rearrange("p (e h x) -> p e h x", h=HU, e=3) for x in qk]
        z_w = [arena[:, 5120 + 1024 * i:5120 + 1024 * (i + 1)].rearrange("p (h x) -> p h x", h=H)
               for i in range(2)]
        wT = arena[:, 7168:8192].rearrange("p (h x) -> p h x", h=H)
        a_out = [arena[:, 8192 + 512 * i:8192 + 512 * (i + 1)] for i in range(2)]
        sc = [arena[:, 9216 + 256 * i:9216 + 256 * (i + 1)].rearrange("p (a x) -> p a x", x=32) for i in range(2)]
        small = arena[:, 9728:10240]
        ar = small[:, 0:64]
        ar_sq = small[:, 64:128]
        mag = small[:, 128:160].rearrange("p (h m) -> p h m", m=N)
        top = small[:, 160:168]
        ex = small[:, 192:224].rearrange("p (h m) -> p h m", m=N)
        total = small[:, 224:232]
        inv = small[:, 232:240]
        wgt = small[:, 240:272].rearrange("p (h m) -> p h m", m=N)
        root = small[:, 272:304].rearrange("p (h m) -> p h m", m=N)
        quot = small[:, 304:336].rearrange("p (h m) -> p h m", m=N)
        v_nat = arena[:, 10240:11264].rearrange("p (s x) -> p s x", s=2)

        par_in = sem("par_in")
        w_in = sem("w_in")
        w_hi_done = sem("w_hi_done")
        w_lo_done = sem("w_lo_done")
        raw_in = [sem(f"raw_in{i}") for i in range(3)]
        cent = sem("cent")
        normed = sem("normed")
        gelu_done = sem("gelu_done")
        act_hi_done = sem("act_hi_done")
        act_lo_done = sem("act_lo_done")
        used = sem("used")
        evac = sem("evac")
        tile_done = sem("tile_done")
        tile_evac = sem("tile_evac")
        stored = [sem(f"stored{i}") for i in range(2)]
        acc_done = sem("acc_done")
        sq_done = sem("sq_done")
        acc2_done = sem("acc2_done")
        ones_done = sem("ones_done")
        zeroed = sem("zeroed")
        sums_done = sem("sums_done")
        st_mean = sem("st_mean")
        st_msq = sem("st_msq")
        st_var = sem("st_var")
        st_eps = sem("st_eps")
        st_root = sem("st_root")
        st_recip = sem("st_recip")
        st_saved = sem("st_saved")
        st_back = sem("st_back")
        q_stored = [sem(f"q_stored{i}") for i in range(2)]

        ident_z = sem("ident_z")
        masks = sem("masks")
        v_in = sem("v_in")
        qk_in = [sem(f"qk_in{i}") for i in range(2)]
        ki_in = [sem(f"ki_in{i}") for i in range(2)]
        negated = sem("negated")
        scores_done = sem("scores_done")
        diag_done = sem("diag_done")
        masked = sem("masked")
        ar_done = sem("ar_done")
        ar_sq_done = sem("ar_sq_done")
        mag2_done = sem("mag2_done")
        mag_ln = sem("mag_ln")
        mag_done = sem("mag_done")
        root_inv = sem("root_inv")
        quot_done = sem("quot_done")
        root_done = sem("root_done")
        top_done = sem("top_done")
        diff_done = sem("diff_done")
        exp_done = sem("exp_done")
        total_done = sem("total_done")
        inv_done = sem("inv_done")
        wgt_done = sem("wgt_done")
        z_done = sem("z_done")
        vT_done = sem("vT_done")
        v_nat_done = sem("v_nat_done")
        zT_done = sem("zT_done")
        wT_done = [sem(f"wT_done{i}") for i in range(2)]
        pv_done = sem("pv_done")
        o_hi_done = sem("o_hi_done")
        o_lo_done = sem("o_lo_done")
        wo_done = sem("wo_done")
        a_out_done = sem("a_out_done")
        a_stored = [sem(f"a_stored{i}") for i in range(2)]

        WI_FIRST = {1: 0, 2: 1, 3: 2}
        WI_LOOP = 3
        WI_END = {0: 10, 1: 11}
        wi_late = [wi_raw, arena[:, 2048:3072], arena[:, 3072:4096], arena[:, 5120:6144]]
        wi_in = sem("wi_in")
        wi_hi_done = sem("wi_hi_done")
        wi_lo_done = sem("wi_lo_done")

        z = arena[:, 0:4096].rearrange("p (q e n x) -> p q e n x", q=4, e=2, n=N)
        a_raw = arena[:, 4096:5120].rearrange("p (s c x) -> p s c x", s=2, c=DC)
        z_sq = [arena[:, 5120 + 512 * i:6144 + 512 * i].rearrange("p (e n x) -> p e n x", e=2, n=N)
                for i in range(2)]
        m2 = [z_sq[0][:, 0], z_sq[1][:, 1]]
        rt = [arena[:, 6656 + 512 * i:7168 + 512 * i].rearrange("p (n x) -> p n x", n=N) for i in range(2)]
        un = arena[:, 7680:8704].rearrange("p (e n x) -> p e n x", e=2, n=N)
        t_r = arena[:, 8704:9472].rearrange("p (k x) -> p k x", k=6)
        t_i = arena[:, 9472:10240].rearrange("p (k x) -> p k x", k=6)
        sup = arena[:, 10240:11264].rearrange("p (e x) -> p e x", e=2)
        sup_flat = arena[:, 10240:11264]
        PAIRS = [(i, i + d) for d in range(1, N) for i in range(N - d)]
        AT = {1: (0, 3), 2: (3, 5), 3: (5, 6)}
        nrm = sb("nrm", [P, 2])
        tiny = sb("tiny", [P, 2])
        ids_sb = sb("ids_sb", [P, TILES_B, N], I32)
        strength = sb("strength", [P, TILES_B, N * N])
        ids_in = sem("ids_in")
        strength_in = sem("strength_in")
        a_in = sem("a_in")
        a_hi_done = sem("a_hi_done")
        a_lo_done = sem("a_lo_done")
        neg_lo_done = sem("neg_lo_done")
        int_done = sem("int_done")
        z_out = sem("z_out")
        z_sq_done = sem("z_sq_done")
        early_sq = sem("early_sq")
        early_m2 = sem("early_m2")
        early_rinv = sem("early_rinv")
        m2_done = sem("m2_done")
        ln_done = sem("ln_done")
        rinv_done = sem("rinv_done")
        ur_done = sem("ur_done")
        ui_done = sem("ui_done")
        tr_done = sem("tr_done")
        ti_done = sem("ti_done")
        t_done = sem("t_done")
        zero_marked = sem("zero_marked")
        t_first = sem("t_first")
        ti_first = sem("ti_first")
        t_marked = sem("t_marked")
        t_mult = sem("t_mult")
        c_round = sem("c_round")
        prod_done = sem("prod_done")
        half_sum = sem("half_sum")
        sup_done = sem("sup_done")
        nrm_sq = sem("nrm_sq")
        nrm_ln = sem("nrm_ln")
        nrm_inv = sem("nrm_inv")
        scaled = sem("scaled")
        supT_done = sem("supT_done")
        supT_out = sem("supT_out")
        sup_stored = sem("sup_stored")

        mr_st = [arena[:, 2048 + 1024 * i:3072 + 1024 * i] for i in range(2)]
        top_x = [arena[:, 4096 + 512 * i:4608 + 512 * i] for i in range(2)]
        post = arena[:, 5120:9216].rearrange("p (c x) -> p c x", c=DC)
        m_sq = arena[:, 9216:10240]
        x_t = [arena[:, 10240 + 512 * i:10752 + 512 * i] for i in range(2)]
        post_sq = arena[:, 9216:11264].rearrange("p (c x) -> p c x", c=DC)
        sup_ring = [arena[:, at:at + 1024].rearrange("p (e x) -> p e x", e=2) for at in (4096, 2048, 3072)]
        sup_in = [sem(f"sup_in{i}") for i in range(3)]
        m_hi_done = sem("m_hi_done")
        m_lo_done = sem("m_lo_done")
        top_in = [sem(f"top_in{i}") for i in range(2)]
        meas_done = sem("meas_done")
        m_sq_done = sem("m_sq_done")
        amp2_done = sem("amp2_done")
        amp_done = sem("amp_done")
        amp_hi_done = sem("amp_hi_done")
        amp_lo_done = sem("amp_lo_done")
        post_done = sem("post_done")
        post_out = sem("post_out")
        post_sq_done = sem("post_sq_done")
        post_sums = sem("post_sums")
        p_mean = sem("p_mean")
        p_msq = sem("p_msq")
        p_var = sem("p_var")
        p_eps = sem("p_eps")
        p_root = sem("p_root")
        p_inv = sem("p_inv")
        p_cent = sem("p_cent")
        p_normed = sem("p_normed")
        z_gelu = sem("z_gelu")
        z_hi_done = sem("z_hi_done")
        z_lo_done = sem("z_lo_done")
        top1_done = sem("top1_done")
        x_done = sem("x_done")
        h1_hi_done = sem("h1_hi_done")
        h1_lo_done = sem("h1_lo_done")
        top2_done = sem("top2_done")
        h2_done = sem("h2_done")
        y_done = sem("y_done")
        y_out = sem("y_out")
        y_stored = sem("y_stored")

        def acc_at(mt):
            return ps_st[mt // 2][:, (mt % 2) * 512:(mt % 2 + 1) * 512]

        def cols_of(half):
            return slice(half * HALF, (half + 1) * HALF)

        SETS = ["x", "h_r", "h_i", "s_r", "s_i"]
        SRC = {"x": xT, "h_r": hT["r"], "h_i": hT["i"], "s_r": sT["r"], "s_i": sT["i"]}
        LAST = {1: G_TOP + DC - 1, 2: G_L2["r"] + KC - 1, 3: G_L2["i"] + KC - 1}
        STAGES = [("l1_r", 0, KC), ("l1_i", KC, KC), ("top1x", G_TOP, DC), ("l2_r", G_L2["r"], KC),
                  ("l2_i", G_L2["i"], KC)]
        BIAS = {"l1_r": "b1_r", "l1_i": "b1_i", "top1x": "b_top1", "l2_r": "b2_r", "l2_i": "b2_i"}
        OUTS = {"l1_r": hT["r"], "l1_i": hT["i"], "top1x": topT, "l2_r": sT["r"], "l2_i": sT["i"]}
        NEXT_SET = {"top1x": 1, "l2_r": 2, "l2_i": 3}

        def blocks(eng, stage, step):
            name, g0, n = stage
            lo, hi = g0 // 2, (g0 + n) // 2
            first = lo + (name in ("l1_r", "l1_i", "top1x", "l2_r", "l2_i"))
            last = hi - (name in NEXT_SET)
            for j in range(lo, first):
                for p in range(2):
                    step(j, p)
            if first < last:
                with eng.Fori(first, last) as j:
                    for p in range(2):
                        step(j, p)
            for j in range(max(last, first), hi):
                for p in range(2):
                    step(j, p)

        def is_block(j, p, g):
            return isinstance(j, int) and 2 * j + p == g

        def wait_chunk_free(eng, k, c):
            if k in LAST:
                eng.wait_ge(used, KC * LAST[k] + c + 1)
            if k == 4:
                eng.wait_ge(tile_done, TILES_Q - N + c // DC + 1)

        def groups(eng, step):
            for g in range(4):
                step(0, g)
            with eng.Fori(1, TILES_B) as t:
                for g in range(4):
                    step(t, g)
            for g in range(2):
                step(TILES_B, g)

        def tiles(eng, step):
            step(0)
            with eng.Fori(1, TILES_B - 2) as t:
                step(t)
            step(TILES_B - 2)
            step(TILES_B - 1)

        block = ctx.enter_context(nc.Block())

        @block.sync
        def _(sp):
            sp.dma_start(par[:, :], cols).then_inc(par_in, 16)

            def weights(src, g):
                sp.wait_ge(w_lo_done, g)
                sp.dma_start(w_raw, src).then_inc(w_in, 16)

            def chunks(k):
                if k == 1:
                    sp.wait_ge(sums_done, 2)
                    sp.wait_ge(st_saved, 16)
                    sp.dma_start(misc[1], stat_rows.to_broadcast([P, 2 * B])).then_inc(st_back, 16)
                    sp.wait_ge(acc2_done, 2 * KC)
                if k in (1, 3):
                    for s in range(2):
                        sp.wait_ge(stored[s], 8 * (G_TOP if k == 1 else G_L2["i"]))
                if k in (2, 4):
                    for s in range(2):
                        sp.wait_ge(stored[s], 8 * (G_TOP if k == 2 else G_END))
                for c in range(KC):
                    q = KC * k + c
                    if q >= 3:
                        sp.wait_ge(act_lo_done, q - 2)
                    sp.dma_start(ring[q % 3], SRC[SETS[k]][c]).then_inc(raw_in[q % 3], 16)

            def stage(name, g0, n, k=None):
                weights(w[name][0], g0)
                if k is not None:
                    chunks(k)
                with sp.Fori(1, n) as m:
                    weights(w[name][m], m + g0)

            stage(*STAGES[0], 0)
            stage(*STAGES[1])
            stage(*STAGES[2])
            stage(*STAGES[3], 1)
            stage(*STAGES[4], 2)

            def half_blocks(s, k):
                u0 = 0 if s == "r" else 6

                def half_block(u, m, e):
                    sp.wait_ge(w_lo_done, G_END + u)
                    sp.dma_start(w_raw[:, 0:BLK // 2],
                                 w["qkv_" + s][m, :, e * (BLK // 2):(e + 1) * (BLK // 2)]).then_inc(w_in, 16)

                half_block(u0, 0, 0)
                chunks(k)
                half_block(u0 + 1, 0, 1)
                with sp.Fori(1, 3) as m:
                    for e in range(2):
                        half_block(2 * m + (u0 + e), m, e)

            half_blocks("r", 3)
            half_blocks("i", 4)

            def load_wo(s):
                sp.wait_ge(w_lo_done, G_WO + s)
                sp.dma_start(w_raw, w["o"][s]).then_inc(w_in, 16)

            load_wo(0)

            def load_unit(t, g, hh):
                e = hh
                if not (isinstance(t, int) and t == 0 and g == 0):
                    sp.wait_ge(scores_done, 8 * t + (2 * g + hh - 1))
                cs = bass.ds((t * 4 + g) * P, P)
                keys = {s: qkT[s][hh, 1].rearrange("(h d) x -> d h x", d=HD)[:, :, cs] for s in "ri"}
                both = {s: qkT[s][hh].rearrange("m (h d) x -> d (m h) x", d=HD)[:, :, cs] for s in "ri"}
                sp.dma_start(qkk[e][0:64, 2], keys["i"]).then_inc(ki_in[e], 16)
                sp.dma_start(qkk[e][64:128, 2], keys["r"]).then_inc(qk_in[e], 16)
                for s, lo in (("r", 0), ("i", 64)):
                    sp.dma_start(qkk[e][lo:lo + 64, 0:2].rearrange("p e h x -> p (e h) x"), both[s])\
                        .then_inc(qk_in[e], 16)

            def load_v(t, g):
                if not (isinstance(t, int) and 4 * t + g == 0):
                    sp.wait_ge(vT_done, 8 * t + 2 * g)
                for si, s in enumerate("ri"):
                    src = valT[s].rearrange("(c p) x -> p c x", p=P)[:, :, bass.ds((t * 4 + g) * P, P)]
                    sp.dma_start(v_raw[:, si], src).then_inc(v_in, 16)

            def load_wi(b):
                sp.wait_ge(wi_lo_done, b)
                sp.dma_start(wi_raw, w["int"][b]).then_inc(wi_in, 16)

            sp.wait_ge(act_lo_done, 5 * KC)
            sp.wait_ge(q_stored[0], 16 * 3 * DC * 2)

            def step(t, g):
                first = isinstance(t, int) and t == 0
                if not (isinstance(t, int) and t == TILES_B):
                    for hh in range(2):
                        load_unit(t, g, hh)
                if first and g == 0:
                    load_wo(1)
                    sp.wait_ge(q_stored[1], 16 * 3 * DC * 2)
                if first and g == 1:
                    sp.wait_ge(w_lo_done, G_WO + 2)
                if not (first and g == 0 or isinstance(t, int) and t == TILES_B and g == 1):
                    load_v(t, g - 1)
                if first and g > 0:
                    load_wi(WI_FIRST[g])
                if isinstance(t, int) and t == TILES_B:
                    load_wi(WI_END[g])
                if not isinstance(t, int) and g == 1:
                    load_wi(t + (WI_LOOP - 1))

            groups(sp, step)

            sp.wait_ge(scores_done, 2 * GROUPS)
            sp.wait_ge(zT_done, 2 * GROUPS)
            sp.wait_ge(wi_lo_done, 12)
            for b in range(12, 16):
                sp.dma_start(wi_late[b - 12], w["int"][b]).then_inc(wi_in, 16)
            for e in range(2):
                sp.wait_ge(a_stored[e], 16 * DC * TILES_B)

            def load_a(t, pos, bs):
                n = (pos + 1) % N
                if t or pos:
                    sp.wait_ge(a_lo_done, 4 * t + pos)
                    sp.wait_ge(neg_lo_done, 4 * t + pos)
                for si, s in enumerate("ri"):
                    src = attnT[s].rearrange("c p n b -> p n c b")[:, n, :, bs]
                    sp.dma_start(a_raw[:, si], src).then_inc(a_in, 16)

            for t in range(TILES_B):
                bs = slice(t * P, (t + 1) * P)
                for pos in range(N):
                    load_a(t, pos, bs)

            sp.wait_ge(sup_done, 4 * TILES_B - 2)
            for k in range(2):
                sp.wait_ge(w_lo_done, G_WO + 2 + k)
                sp.dma_start(w_raw, w["meas"][k]).then_inc(w_in, 16)
            for u in range(2 * DC):
                half, c = u // DC, u % DC
                if u < 3:
                    sp.wait_ge(neg_lo_done, 4 * TILES_B)
                    sp.wait_ge(a_lo_done, 4 * TILES_B)
                    sp.wait_ge(sup_done, 4 * TILES_B + min(0, u - 2))
                    sp.wait_ge(sup_stored, 32 * (TILES_B // 2))
                else:
                    sp.wait_ge(m_lo_done, u - 2)
                if half:
                    sp.wait_ge(sup_stored, 32 * TILES_B)
                sp.dma_start(sup_ring[u % 3], supT[:, c].rearrange("e p b -> p e b")[:, :, cols_of(half)])\
                    .then_inc(sup_in[u % 3], 16)
            for k, src in enumerate((w["post"], w["top1z"], w["top2"])):
                sp.wait_ge(w_lo_done, G_WO + 4 + k)
                sp.dma_start(w_raw[:, 0:src.shape[1]], src).then_inc(w_in, 16)
            sp.wait_ge(m_lo_done, 2 * DC)
            for u in range(2 * DC):
                if u >= 2:
                    sp.wait_ge(x_done, u - 1)
                half, mt = u // DC, u % DC
                sp.dma_start(top_x[u % 2], topT[mt][:, half * HALF:(half + 1) * HALF]).then_inc(top_in[u % 2], 16)

        @block.scalar
        def _(act):
            act.wait_ge(par_in, 16)

            def split(j, p):
                act.wait_ge(w_in, 32 * j + 16 * p + 16)
                if not (isinstance(j, int) and j == 0):
                    act.wait_ge(used, 2 * KC * j + KC * (p - 1))
                act.activation(w_hi[:, p, :], w_raw, ACT.Copy).then_inc(w_hi_done, 1)

            def chunks(k, some=range(KC)):
                name = SETS[k]
                for c in some:
                    q = KC * k + c
                    if name[0] == "h":
                        act.wait_ge(normed, KC * (k - 1) + c + 1)
                        g0, b0 = COLS["g_" + name[2]] + c, COLS["be_" + name[2]] + c
                        act.activation(ring[q % 3], ring[q % 3], ACT.Gelu, bias=par[:, b0:b0 + 1],
                                       scale=par[:, g0:g0 + 1]).then_inc(gelu_done, 1)
                        act.wait_ge(gelu_done, KC * (k - 1) + c + 1)
                    else:
                        act.wait_ge(raw_in[q % 3], 16 * (q // 3 + 1))
                    wait_chunk_free(act, k, c)
                    act.activation(act_hi[:, c, :], ring[q % 3], ACT.Copy).then_inc(act_hi_done, 1)

            def take_out(j, p, name, g0):
                act.wait_ge(used, 2 * KC * j + KC * (p + 1))
                if not (isinstance(j, int) and j == 0):
                    act.wait_ge(stored[p], 16 * j)
                    if name in ("l1_r", "l1_i"):
                        act.wait_ge(acc_done, 2 * j + p - 1)
                        act.wait_ge(acc2_done, 2 * j + p - 1)
                    if name == "top1x":
                        act.wait_ge(acc_done, 2 * KC)
                        act.wait_ge(acc2_done, 2 * KC)
                act.activation(hout[p], ps[p][:, :], ACT.Identity,
                               bias=par[:, bass.ds(2 * j + (p + COLS[BIAS[name]] - g0), 1)]).then_inc(evac, 1)

            def half_block_split(u, e, tiles=None):
                act.wait_ge(w_in, 16 * u + 16 * G_END + 16)
                if tiles is None:
                    act.wait_ge(used, KC * (G_END - (1 - e)))
                else:
                    act.wait_ge(tile_done, tiles)
                act.activation(w_hi[:, e, 0:BLK // 2], w_raw[:, 0:BLK // 2], ACT.Copy).then_inc(w_hi_done, 1)

            split(0, 0)
            chunks(0)
            for stage in STAGES:
                name, g0, n = stage

                def step(j, p):
                    if is_block(j, p, G_END - 1):
                        half_block_split(0, 0)
                    elif p == 0:
                        split(j, 1)
                    else:
                        split(j + 1, 0)
                    if name in NEXT_SET and is_block(j, p, g0 + n - 1):
                        chunks(NEXT_SET[name])
                    take_out(j, p, name, g0)
                    if is_block(j, p, KC) or is_block(j, p, G_TOP):
                        act.wait_ge(st_eps, 1 + (g0 == G_TOP))
                        act.activation(st[:, B:2 * B], st[:, B:2 * B], ACT.Sqrt).then_inc(st_root, 1)

                blocks(act, stage, step)

            for s in range(2):
                act.wait_ge(stored[s], 8 * G_END)
            for si, s in enumerate("ri"):
                T0 = TILES_Q * si

                def tile(m, mt, half, n):
                    i = (mt * 2 + half) * N + n
                    u = 2 * N * DC * m + (T0 + i)
                    act.wait_ge(tile_done, u + 1)
                    if n == 0:
                        act.wait_ge(q_stored[half], 16 * DC * m + 16 * (DC * 3 * si + mt))
                    c0 = COLS["bqkv_" + s] + mt
                    act.activation(qout[half][:, :, n], ps_st[i // 2 % 2][:, (i % 2) * HALF:(i % 2 + 1) * HALF],
                                   ACT.Identity, bias=par[:, bass.ds(DC * m + c0, 1)]).then_inc(tile_evac, 1)

                def half_tiles(m, e, then_chunks=False):
                    for mt in range(2 * e, 2 * e + 2):
                        for half in range(2):
                            for n in range(N):
                                tile(m, mt, half, n)
                                if then_chunks and mt == DC - 1 and half == 1:
                                    chunks(4, range(n * DC, (n + 1) * DC))

                def matrix(m, last):
                    if isinstance(m, int) and m == 0 and si == 0:
                        half_block_split(1, 1)
                    else:
                        half_block_split(2 * m + (6 * si + 1), 1, 32 * m + T0)
                    half_tiles(m, 0)
                    if not last:
                        half_block_split(2 * m + (6 * si + 2), 0, 32 * m + (T0 + 16))
                    elif si == 0:
                        half_block_split(6, 0, T0 + 80)
                    half_tiles(m, 1, last and si == 0)

                matrix(0, False)
                matrix(1, False)
                matrix(2, True)

            act.wait_ge(tile_done, 2 * TILES_Q)

            def split_wo(s):
                act.wait_ge(w_in, 16 * (G_WO + s + 1))
                act.activation(w_hi[:, s, :], w_raw, ACT.Copy).then_inc(w_hi_done, 1)

            act.add_instruction(mybir.InstLoadActFuncSet(name=nc.get_next_instruction_name(),
                                                         act_func_set_id=LN_EXP_SET, engine=act.engine))
            split_wo(0)
            for half in range(2):
                act.wait_ge(q_stored[half], 16 * 3 * DC * 2)

            def split_wi(b, late=False):
                act.wait_ge(wi_in, 16 * 16 if late else 16 * b + 16)
                raw, at = (wi_late[b - 12], b - 12) if late else (wi_raw, b + DC)
                act.activation(act_hi[:, at, :], raw, ACT.Copy).then_inc(wi_hi_done, 1)

            def take_values(t, g):
                start = isinstance(t, int) and t == 0
                k1 = 4 * t + g
                for si in range(2):
                    act.wait_ge(vT_done, 2 * k1 + (si - 1))
                    if not (start and g == 1):
                        act.wait_ge(pv_done, 2 * k1 - 2)
                    act.activation(v_nat[:, si], ps_st[0][:, si * 512:(si + 1) * 512],
                                   ACT.Copy).then_inc(v_nat_done, 1)

            def step(t, g):
                start, end = isinstance(t, int) and t == 0, isinstance(t, int) and t == TILES_B
                k1 = 4 * t + (g - 1)
                for hh in range(2):
                    if not end:
                        act.wait_ge(scores_done, 8 * t + (2 * g + hh + 1))
                        if not (start and g == 0):
                            act.wait_ge(ar_done, 8 * t + (2 * g + hh - 1))
                        src = ps[hh][:, :].rearrange("p (a x) -> p a x", x=P)
                        for qd in range(4):
                            rows = slice(32 * qd, 32 * qd + 32)
                            act.activation(sc[hh][rows], src[rows, :, rows], ACT.Copy).then_inc(diag_done, 1)
                    if hh == 0 and not (start and g < 2):
                        act.wait_ge(zT_done, 2 * k1)
                        if not (start and g == 2):
                            act.wait_ge(pv_done, 2 * k1 - 2)
                        act.activation(wT[:, 4:8, :], ps_st[0][:, 512:].rearrange("p (h x) -> p h x", x=P),
                                       ACT.Copy).then_inc(wT_done[1], 1)
                if not (start and g < 2):
                    for si in range(2):
                        act.wait_ge(pv_done, 2 * k1 + (si - 1))
                        if g == 2 and not start:
                            act.wait_ge(wo_done, 8 * t)
                        cs = slice((g + 2) % 4 * P, ((g + 2) % 4 + 1) * P)
                        act.activation(act_hi[:, 0:DC, si * HALF + cs.start:si * HALF + cs.stop],
                                       ps_st[1][:, si * 512:(si + 1) * 512].rearrange("p (c x) -> p c x", c=DC),
                                       ACT.Copy).then_inc(o_hi_done, 1)
                if not end:
                    act.wait_ge(mag2_done, 4 * t + (g + 1))
                    act.activation(root, mag, ACT.Ln).then_inc(mag_ln, 1)
                    act.wait_ge(mag_ln, 4 * t + (g + 1))
                    act.activation(root, root, ACT.Exp, scale=0.5).then_inc(mag_done, 1)
                    if (g > 0) if start else (g != 1):
                        take_values(t, g)
                    act.wait_ge(diff_done, 4 * t + (g + 1))
                    act.activation(ex, ex, ACT.Exp, scale=0.5 * HD ** -0.5).then_inc(exp_done, 1)
                if end:
                    split_wi(WI_END[g])
                if g == 1 and not start:
                    for i in range(2 * DC):
                        act.wait_ge(wo_done, 8 * t + (i - 7))
                        if i >= 2 or not (isinstance(t, int) and t == 1):
                            act.wait_ge(a_stored[i % 2], 64 * t + (16 * (i // 2) - 64))
                        c0 = COLS["bo_" + "ri"[i // DC]] + i % DC
                        act.activation(a_out[i % 2].rearrange("p (n b) -> p b n", n=N),
                                       ps_st[0][:, (i % 2) * 512:(i % 2 + 1) * 512]
                                       .rearrange("p (b n) -> p b n", n=N), ACT.Identity,
                                       bias=par[:, c0:c0 + 1]).then_inc(a_out_done, 1)
                        act.wait_ge(a_out_done, 8 * t + (i - 7))
                        act.dma_start(attnT["ri"[i // DC]][i % DC][:, :, bass.ds((t - 1) * P, P)],
                                      a_out[i % 2].rearrange("p (n b) -> p n b", n=N)).then_inc(a_stored[i % 2], 16)
                if end and g == 0 or not start and not end and g == 1:
                    take_values(t, g)
                if start and g == 0:
                    split_wo(1)
                if start and g > 0:
                    split_wi(WI_FIRST[g])
                if not isinstance(t, int) and g == 1:
                    split_wi(t + (WI_LOOP - 1))

            groups(act, step)

            act.wait_ge(wo_done, 2 * DC * TILES_B)

            def split_a(t, pos):
                e = pos % 2
                act.wait_ge(a_in, 128 * t + 32 * (pos + 1))
                if not (isinstance(t, int) and t == 0 and pos < 2):
                    act.wait_ge(int_done, 4 * t + (pos - 1))
                act.activation(w_hi[:, e, 0:1024], a_raw.rearrange("p s c x -> p (s c x)"),
                               ACT.Copy).then_inc(a_hi_done, 1)
                act.activation(w_hi[:, e, 1024:1536], a_raw[:, 1].rearrange("p c x -> p (c x)"),
                               ACT.Copy, scale=-1.0).then_inc(a_hi_done, 1)

            def take_z(t, pos, quarters):
                lo, hi = quarters
                acc_ri = acc_of[pos].rearrange("p (e q x) -> p q e x", e=2, q=4)
                act.activation(z[:, lo:hi, :, (pos + 1) % N, :], acc_ri[:, lo:hi], ACT.Copy).then_inc(z_out, 1)

            def square(t, q, ns=slice(0, N), done=z_sq_done):
                if not (isinstance(t, int) and 4 * t + q == 0):
                    act.wait_ge(m2_done, 4 * t + q)
                if not (isinstance(t, int) and 4 * t + q < 2):
                    act.wait_ge(ti_done, 4 * t + (q - 1))
                    if q != 1:
                        act.wait_ge(t_marked, 3 * t + max(q - 1, 0))
                act.activation(z_sq[q % 2][:, :, ns], z[:, q, :, ns], ACT.Square).then_inc(done, 1)

            def one_over(t, q, ns=slice(0, N), done=rinv_done):
                if not (isinstance(t, int) and 4 * t + q < 2):
                    act.wait_ge(prod_done, 4 * t + (q - 1))
                act.activation(rt[q % 2][:, ns], m2[q % 2][:, ns], ACT.Ln, bias=tiny[:, 0:1]).then_inc(ln_done, 1)
                act.wait_ge(ln_done, 5 * t + (q + (1 if done is early_rinv else 2)))
                act.activation(rt[q % 2][:, ns], rt[q % 2][:, ns], ACT.Exp, scale=-0.5).then_inc(done, 1)

            def magnitudes(t, q):
                act.wait_ge(z_out, 8 * t + (8 if q == 3 else 4))
                square(t, q)

            def inverses(t, q):
                act.wait_ge(m2_done, 4 * t + (q + 1))
                one_over(t, q)

            def norm(t1):
                act.wait_ge(sup_done, 4 * t1)
                act.wait_ge(m2_done, 4 * t1)
                act.activation(z_sq[1].rearrange("p e n x -> p (e n x)"), sup_flat, ACT.Square,
                               accum_out=nrm[:, 0:1]).then_inc(nrm_sq, 1)
                act.wait_ge(nrm_sq, t1)
                act.activation(nrm[:, 0:1], nrm[:, 0:1], ACT.Ln, bias=tiny[:, 1:2]).then_inc(nrm_ln, 1)
                act.wait_ge(nrm_ln, t1)
                if not (isinstance(t1, int) and t1 == 1):
                    act.wait_ge(scaled, t1 - 1)
                act.activation(nrm[:, 1:2], nrm[:, 0:1], ACT.Exp, scale=-0.5).then_inc(nrm_inv, 1)

            def store_sup(t1):
                for e in range(2):
                    act.wait_ge(supT_done, 2 * t1 + (e - 1))
                    if e == 0:
                        act.wait_ge(supT_done, 2 * t1)
                    act.activation(sup[:, e], ps_st[1][:, e * 512:(e + 1) * 512],
                                   ACT.Copy).then_inc(supT_out, 1)
                    act.wait_ge(supT_out, 2 * t1 + (e - 1))
                    act.dma_start(supT[e].rearrange("c p b -> p c b")[:, :, bass.ds((t1 - 1) * P, P)],
                                  sup[:, e].rearrange("p (c x) -> p c x", c=DC)).then_inc(sup_stored, 16)

            def split_w(k, e, n=BLK):
                act.wait_ge(w_in, 16 * (G_WO + 3 + k))
                act.activation(w_hi[:, e, 0:n], w_raw[:, 0:n], ACT.Copy).then_inc(w_hi_done, 1)

            acc_of = [ps[0][:, :], ps[1][:, :], ps_st[0][:, :], ps_st[1][:, :]]
            for t, pos in [(0, 0), (0, 1), (0, 2), (0, 3), (1, 0)]:
                split_a(t, pos)
                if t == pos == 0:
                    for b in range(12, 16):
                        split_wi(b, True)
            act.wait_ge(wi_lo_done, 16)

            def step(t):
                start, last = isinstance(t, int) and t == 0, isinstance(t, int) and t == TILES_B - 1
                if not start:
                    act.wait_ge(sup_done, 4 * t - 1)
                for pos in range(N - 1):
                    act.wait_ge(int_done, 4 * t + (pos + 1))
                    take_z(t, pos, (0, 3))
                act.wait_ge(z_out, 8 * t + 3)
                square(t, 0, slice(1, N), early_sq)
                act.wait_ge(early_m2, t + 1)
                one_over(t, 0, slice(1, N), early_rinv)
                act.wait_ge(int_done, 4 * t + N)
                take_z(t, N - 1, (0, 3))
                act.wait_ge(z_out, 8 * t + 4)
                square(t, 0, slice(0, 1))
                act.wait_ge(m2_done, 4 * t + 1)
                one_over(t, 0, slice(0, 1))
                if not start:
                    act.wait_ge(sup_done, 4 * t)
                for pos in range(N):
                    take_z(t, pos, (3, 4))
                if not last:
                    split_a(t + 1, 1)
                if not start:
                    norm(t)
                magnitudes(t, 1)
                inverses(t, 1)
                magnitudes(t, 2)
                inverses(t, 2)
                if not last:
                    split_a(t + 1, 2)
                if not start:
                    store_sup(t)
                magnitudes(t, 3)
                inverses(t, 3)
                if last:
                    for k in range(2):
                        split_w(k, k)
                if not last:
                    split_a(t + 1, 3)
                if not (isinstance(t, int) and t >= TILES_B - 2):
                    split_a(t + 2, 0)

            tiles(act, step)

            def split_sup(u):
                half, c = u // DC, u % DC
                act.wait_ge(sup_in[u % 3], 16 * (u // 3 + 1))
                act.activation(act_hi[:, c:c + DC + 1:DC, cols_of(half)], sup_ring[u % 3], ACT.Copy)\
                    .then_inc(m_hi_done, 1)
                act.activation(act_hi[:, c + 2 * DC, cols_of(half)], sup_ring[u % 3][:, 1], ACT.Copy,
                               scale=-1.0).then_inc(m_hi_done, 1)

            split_sup(0)
            split_sup(1)
            norm(TILES_B)
            split_sup(2)
            split_sup(3)
            store_sup(TILES_B)
            for u in range(DC, 2 * DC):
                split_sup(u)

            for u in range(2 * DC):
                half, mt = u // DC, u % DC
                act.wait_ge(meas_done, u + 1)
                if u:
                    act.wait_ge(amp2_done, u)
                act.activation(m_sq, ps[u % 2][:, :], ACT.Square).then_inc(m_sq_done, 1)
                act.wait_ge(amp2_done, u + 1)
                act.activation(x_t[u % 2], x_t[u % 2], ACT.Sqrt).then_inc(amp_done, 1)
                act.wait_ge(amp_done, u + 1)
                act.activation(act_hi[:, 3 * DC + mt, cols_of(half)], x_t[u % 2], ACT.Copy).then_inc(amp_hi_done, 1)
            split_w(2, 0)
            act.wait_ge(amp_lo_done, 2 * DC)
            for half in range(2):
                for mt in range(DC):
                    u = half * DC + mt
                    act.wait_ge(post_done, u + 1)
                    c0 = COLS["post_b"] + mt
                    act.activation(post[:, mt, cols_of(half)], acc_at(mt), ACT.Identity,
                                   bias=par[:, c0:c0 + 1]).then_inc(post_out, 1)
                    act.wait_ge(post_out, u + 1)
                    if half:
                        act.wait_ge(post_sums, 1)
                    act.activation(post_sq[:, mt], post[:, mt, cols_of(half)], ACT.Square).then_inc(post_sq_done, 1)
                if half == 0:
                    split_w(3, 1)
                    act.wait_ge(post_done, DC)
            act.wait_ge(post_done, 2 * DC)
            split_w(4, 0, 2 * DC * P)
            for half in range(2):
                act.wait_ge(p_eps, half + 1)
                act.activation(mr_st[half][:, HALF:], mr_st[half][:, HALF:], ACT.Sqrt).then_inc(p_root, 1)
                for mt in range(DC):
                    u = half * DC + mt
                    act.wait_ge(p_normed, u + 1)
                    g0, b0 = COLS["post_g"] + mt, COLS["post_be"] + mt
                    act.activation(post[:, mt, cols_of(half)], post[:, mt, cols_of(half)], ACT.Gelu,
                                   bias=par[:, b0:b0 + 1], scale=par[:, g0:g0 + 1]).then_inc(z_gelu, 1)
                    act.wait_ge(z_gelu, u + 1)
                    act.activation(act_hi[:, mt, cols_of(half)], post[:, mt, cols_of(half)],
                                   ACT.Copy).then_inc(z_hi_done, 1)
            for half in range(2):
                for mt in range(DC):
                    u = half * DC + mt
                    act.wait_ge(x_done, u + 1)
                    act.activation(act_hi[:, DC + mt, cols_of(half)], x_t[u % 2], ACT.Relu).then_inc(h1_hi_done, 1)
            act.wait_ge(z_lo_done, 2 * DC)
            for half in range(2):
                for mt in range(2):
                    act.wait_ge(top2_done, 2 * half + mt + 1)
                    c0 = COLS["b_top2"] + mt
                    act.activation(post[:, mt, cols_of(half)], ps[half][:, mt * 512:(mt + 1) * 512], ACT.Relu,
                                   bias=par[:, c0:c0 + 1]).then_inc(h2_done, 1)
            for half in range(2):
                act.wait_ge(y_done, half + 1)
                act.activation(post[0:1, 2, cols_of(half)], acc_at(half)[0:1, :], ACT.Copy).then_inc(y_out, 1)
            act.wait_ge(y_out, 2)
            act.dma_start(y, post[0:1, 2, :]).then_inc(y_stored, 16)
            act.wait_ge(y_stored, 16)

        @block.vector
        def _(dve):
            dve.memset(misc[1], 0.0).then_inc(zeroed, 1)
            dve.memset(ones[:, :], 1.0).then_inc(ones_done, 1)

            def split(g1, e, n=BLK):
                dve.wait_ge(w_hi_done, g1)
                dve.tensor_tensor(w_lo[:, e, 0:n], w_raw[:, 0:n], w_hi[:, e, 0:n].bitcast(F32),
                                  ALU.subtract).then_inc(w_lo_done, 1)

            def low(k, c):
                q = KC * k + c
                dve.wait_ge(act_hi_done, q + 1)
                dve.tensor_tensor(act_lo[:, c, :], ring[q % 3], act_hi[:, c, :].bitcast(F32),
                                  ALU.subtract).then_inc(act_lo_done, 1)

            def chunks(k):
                name = SETS[k]
                if name[0] != "h":
                    for c in range(KC):
                        low(k, c)
                    return
                norm = misc[1] if name == "h_r" else st
                if name == "h_r":
                    dve.wait_ge(st_back, 16)
                for c in range(KC):
                    q = KC * k + c
                    dve.wait_ge(raw_in[q % 3], 16 * (q // 3 + 1))
                    dve.tensor_tensor(ring[q % 3], ring[q % 3], norm[:, 0:B], ALU.subtract).then_inc(cent, 1)
                    dve.wait_ge(cent, KC * (k - 1) + c + 1)
                    dve.tensor_tensor(ring[q % 3], ring[q % 3], norm[:, B:2 * B], ALU.mult).then_inc(normed, 1)
                    if c:
                        low(k, c - 1)
                low(k, KC - 1)

            def statistics(s):
                dve.wait_ge(sums_done, s + 1)
                if s == 1:
                    dve.wait_ge(st_saved, 16)
                dve.tensor_scalar(st[:, 0:B], ps_st[0][:, :], 1.0 / HID, None, ALU.mult).then_inc(st_mean, 1)
                dve.wait_ge(st_mean, s + 1)
                dve.tensor_tensor(st[:, B:2 * B], st[:, 0:B], st[:, 0:B], ALU.mult).then_inc(st_msq, 1)
                dve.wait_ge(st_msq, s + 1)
                dve.scalar_tensor_tensor(out=st[:, B:2 * B], in0=ps_st[1][:, :], scalar=1.0 / HID,
                                         in1=st[:, B:2 * B], op0=ALU.mult, op1=ALU.subtract).then_inc(st_var, 1)
                dve.wait_ge(st_var, s + 1)
                dve.tensor_scalar(st[:, B:2 * B], st[:, B:2 * B], 0.0, 1e-5, ALU.max, ALU.add).then_inc(st_eps, 1)
                if s == 0:
                    dve.memset(misc[1], 0.0).then_inc(zeroed, 1)
                    dve.wait_ge(zeroed, 2)
                dve.wait_ge(st_root, s + 1)
                dve.reciprocal(st[:, B:2 * B], st[:, B:2 * B]).then_inc(st_recip, 1)

            split(1, 0)
            chunks(0)
            dve.wait_ge(zeroed, 1)
            for stage in STAGES:
                name, g0, n = stage

                def step(j, p):
                    if is_block(j, p, G_END - 1):
                        split(G_END + 1, 0, BLK // 2)
                    else:
                        split(2 * j + (p + 2), 1 - p)
                    if name in NEXT_SET and is_block(j, p, g0 + n - 1):
                        chunks(NEXT_SET[name])
                    if is_block(j, p, KC) or is_block(j, p, G_TOP):
                        statistics(int(g0 == G_TOP))
                    if name in ("l1_r", "l1_i"):
                        dve.wait_ge(evac, 2 * j + (p + 1))
                        if not is_block(j, p, 0):
                            dve.wait_ge(acc_done, 2 * j + p)
                        dve.tensor_tensor(acc, acc, hout[p], ALU.add).then_inc(acc_done, 1)

                blocks(dve, stage, step)
            for si in range(2):
                def matrix(m, last):
                    split(2 * m + (G_END + 6 * si + 2), 1, BLK // 2)
                    if not last:
                        split(2 * m + (G_END + 6 * si + 3), 0, BLK // 2)
                    elif si == 0:
                        split(G_END + 7, 0, BLK // 2)
                        chunks(4)

                matrix(0, False)
                matrix(1, False)
                matrix(2, True)
            split(G_WO + 1, 0)
            for half in range(2):
                dve.wait_ge(q_stored[half], 16 * 3 * DC * 2)
            dve.wait_ge(masks, 7)

            def split_wi(b, late=False):
                dve.wait_ge(wi_hi_done, b + 1)
                raw, at = (wi_late[b - 12], b - 12) if late else (wi_raw, b + DC)
                dve.tensor_tensor(act_lo[:, at, :], raw, act_hi[:, at, :].bitcast(F32),
                                  ALU.subtract).then_inc(wi_lo_done, 1)

            def step(t, g):
                start, end = isinstance(t, int) and t == 0, isinstance(t, int) and t == TILES_B
                k1 = 4 * t + (g - 1)
                G1 = 4 * t + (g + 1)
                if not (start and g < 2):
                    dve.wait_ge(zT_done, 2 * k1 - 1)
                    if not (start and g == 2):
                        dve.wait_ge(pv_done, 2 * k1 - 2)
                    dve.tensor_copy(wT[:, 0:4, :], ps_st[0][:, 0:512].rearrange("p (h x) -> p h x", x=P))\
                       .then_inc(wT_done[0], 1)
                if not end:
                    for hh in range(2):
                        U1 = 8 * t + (2 * g + hh + 1)
                        dve.wait_ge(diag_done, 32 * t + (8 * g + 4 * hh + 4))
                        dve.tensor_tensor(sc[hh], sc[hh], same_row32[:, None, :].to_broadcast([P, 8, 32]),
                                          ALU.mult).then_inc(masked, 1)
                        dve.wait_ge(masked, U1)
                        dve.tensor_reduce(ar[:, 32 * hh:32 * hh + 32].rearrange("p (a m) -> p a m", m=N),
                                          sc[hh].rearrange("p a (b m) -> p a m b", m=N), AX.X, ALU.add)\
                           .then_inc(ar_done, 1)
                    dve.wait_ge(ar_done, 8 * t + (2 * g + 2))
                    dve.tensor_tensor(ar_sq, ar, ar, ALU.mult).then_inc(ar_sq_done, 1)
                    dve.wait_ge(ar_sq_done, G1)
                    sq4 = ar_sq.rearrange("p (h e m) -> p h e m", e=2, m=N)
                    dve.scalar_tensor_tensor(out=mag, in0=sq4[:, :, 0], scalar=1e-8, in1=sq4[:, :, 1],
                                             op0=ALU.add, op1=ALU.add).then_inc(mag2_done, 1)
                if not (start and g < 2):
                    for si in range(2):
                        dve.wait_ge(o_hi_done, 2 * k1 + (si - 1))
                        cs = slice((g + 2) % 4 * P, ((g + 2) % 4 + 1) * P)
                        oc = slice(si * HALF + cs.start, si * HALF + cs.stop)
                        dve.tensor_tensor(act_lo[:, 0:DC, oc],
                                          ps_st[1][:, si * 512:(si + 1) * 512].rearrange("p (c x) -> p c x", c=DC),
                                          act_hi[:, 0:DC, oc].bitcast(F32),
                                          ALU.subtract).then_inc(o_lo_done, 1)
                if not end:
                    dve.wait_ge(mag_done, G1)
                    dve.reciprocal(quot, root).then_inc(root_inv, 1)
                    dve.wait_ge(root_inv, G1)
                    dve.tensor_tensor(quot, quot, mag, ALU.mult).then_inc(quot_done, 1)
                    dve.wait_ge(quot_done, G1)
                    dve.tensor_tensor(mag, quot, root, ALU.add).then_inc(root_done, 1)
                    dve.wait_ge(root_done, G1)
                    dve.tensor_reduce(top, mag, AX.X, ALU.max).then_inc(top_done, 1)
                    dve.wait_ge(top_done, G1)
                    dve.tensor_tensor(ex, mag, top[:, :, None].to_broadcast([P, H, N]),
                                      ALU.subtract).then_inc(diff_done, 1)
                    dve.wait_ge(exp_done, G1)
                    dve.tensor_reduce(total, ex, AX.X, ALU.add).then_inc(total_done, 1)
                    dve.wait_ge(total_done, G1)
                    dve.reciprocal(inv, total).then_inc(inv_done, 1)
                    dve.wait_ge(inv_done, G1)
                    dve.tensor_tensor(wgt, ex, inv[:, :, None].to_broadcast([P, H, N]),
                                      ALU.mult).then_inc(wgt_done, 1)
                    dve.wait_ge(wgt_done, G1)
                    if not (start and g < 2):
                        dve.wait_ge(zT_done, 2 * k1)
                    for e in range(2):
                        hs = slice(4 * e, 4 * e + 4)
                        mm = dve.tensor_tensor(
                            z_w[g % 2][:, hs].rearrange("p h (b m) -> p h b m", m=N),
                            same_row[:, None, :].to_broadcast([P, 4, P]).rearrange("p h (b m) -> p h b m", m=N),
                            wgt[:, hs, None, :].to_broadcast([P, 4, 32, N]), ALU.mult)
                        mm.then_inc(z_done, 1)
                if start and g == 0:
                    split(G_WO + 2, 1)
                if start and g > 0:
                    split_wi(WI_FIRST[g])
                if end:
                    split_wi(WI_END[g])
                if not isinstance(t, int) and g == 1:
                    split_wi(t + (WI_LOOP - 1))

            groups(dve, step)


            def split_a(t, pos):
                e = pos % 2
                dve.wait_ge(a_hi_done, 8 * t + 2 * (pos + 1))
                dve.tensor_tensor(w_lo[:, e, 0:1024], a_raw.rearrange("p s c x -> p (s c x)"),
                                  w_hi[:, e, 0:1024].bitcast(F32), ALU.subtract).then_inc(a_lo_done, 1)

            def quarter(t, q, between=None):
                Q1 = 4 * t + (q + 1)
                C = rt[q % 2]

                def s_(i, j):
                    return strength[:, bass.ds(t, 1), N * i + j]

                dve.wait_ge(rinv_done, Q1)
                dve.tensor_tensor(un[:, 0], z[:, q, 0], C, ALU.mult).then_inc(ur_done, 1)
                dve.wait_ge(ur_done, Q1)
                for d in range(1, N):
                    mm = dve.tensor_tensor(t_r[:, AT[d][0]:AT[d][1]], un[:, 0, 0:N - d], un[:, 0, d:N], ALU.mult)
                mm.then_inc(tr_done, 1)
                dve.wait_ge(tr_done, Q1)
                dve.wait_ge(zero_marked, Q1)
                if q == 0:
                    for d in range(1, N):
                        part = t_r[:, AT[d][0]:AT[d][1]]
                        mm = dve.tensor_tensor(part, part, m2[0][:, 0:N - d], ALU.add)
                    mm.then_inc(t_first, 1)
                    dve.wait_ge(t_first, t + 1)
                if q < 3:
                    for d in range(1, N):
                        part = t_r[:, AT[d][0]:AT[d][1]]
                        mm = dve.tensor_tensor(part, part, m2[q % 2][:, d:N], ALU.add)
                    mm.then_inc(t_marked, 1)
                    dve.wait_ge(t_marked, 3 * t + (q + 1))
                dve.wait_ge(ti_done, Q1)
                dve.tensor_tensor(t_r, t_r, t_i, ALU.add).then_inc(t_done, 1)
                dve.wait_ge(t_done, Q1)
                if between:
                    between()
                for k in range(3):
                    if k:
                        dve.wait_ge(c_round, 12 * t + (3 * q + k))
                    for j in range(N):
                        i = [i for i in range(N) if i != j][k]
                        pair = t_r[:, PAIRS.index((min(i, j), max(i, j)))]
                        if k == 0:
                            mm = dve.tensor_scalar(C[:, j], pair, s_(i, j), s_(j, j), ALU.mult, ALU.add)
                        else:
                            mm = dve.scalar_tensor_tensor(out=C[:, j], in0=pair, scalar=s_(i, j), in1=C[:, j],
                                                          op0=ALU.mult, op1=ALU.add)
                    mm.then_inc(c_round, 1)
                dve.wait_ge(c_round, 12 * t + 3 * (q + 1))
                zq = z[:, q]
                dve.tensor_tensor(zq, zq, C[:, None].to_broadcast([P, 2, N, P]), ALU.mult).then_inc(prod_done, 1)
                dve.wait_ge(prod_done, Q1)
                dve.tensor_tensor(zq[:, :, 0:2], zq[:, :, 0:2], zq[:, :, 2:4], ALU.add).then_inc(half_sum, 1)
                dve.wait_ge(half_sum, Q1)

            def sum_up(t, q):
                if q == 0 and not (isinstance(t, int) and t == 0):
                    dve.wait_ge(sup_stored, 32 * t)
                dve.tensor_tensor(sup[:, :, q * P:(q + 1) * P], z[:, q, :, 0], z[:, q, :, 1],
                                  ALU.add).then_inc(sup_done, 1)

            def norm(t1):
                dve.wait_ge(nrm_inv, t1)
                dve.tensor_scalar(sup, sup, nrm[:, 1:2], None, ALU.mult).then_inc(scaled, 1)

            for t, pos in [(0, 0), (0, 1), (0, 2), (0, 3), (1, 0)]:
                split_a(t, pos)
                if t == pos == 0:
                    for b in range(12, 16):
                        split_wi(b, True)
            dve.wait_ge(strength_in, 16 * TILES_B * N)

            def step(t):
                last = isinstance(t, int) and t == TILES_B - 1

                def between():
                    if not (isinstance(t, int) and t == 0):
                        norm(t)
                    if not last:
                        split_a(t + 1, 1)

                quarter(t, 0, between)
                quarter(t, 1, None if last else lambda: split_a(t + 1, 2))
                for q in range(2):
                    sum_up(t, q)
                quarter(t, 2, None if last else lambda: split_a(t + 1, 3))
                sum_up(t, 2)
                quarter(t, 3, None if isinstance(t, int) and t >= TILES_B - 2 else lambda: split_a(t + 2, 0))
                sum_up(t, 3)

            tiles(dve, step)

            def split_sup(u):
                half, c = u // DC, u % DC
                dve.wait_ge(m_hi_done, 2 * u + 2)
                dve.tensor_tensor(act_lo[:, c + 2 * DC, cols_of(half)],
                                  act_hi[:, c + DC, cols_of(half)].bitcast(F32), sup_ring[u % 3][:, 1], ALU.subtract)
                dve.tensor_tensor(act_lo[:, c:c + DC + 1:DC, cols_of(half)], sup_ring[u % 3],
                                  act_hi[:, c:c + DC + 1:DC, cols_of(half)].bitcast(F32),
                                  ALU.subtract).then_inc(m_lo_done, 1)

            split_sup(0)
            split_sup(1)
            norm(TILES_B)
            for u in range(2, 2 * DC):
                split_sup(u)
            dve.wait_ge(sup_stored, 32 * TILES_B)
            for u in range(2 * DC):
                half, mt = u // DC, u % DC
                dve.wait_ge(m_sq_done, u + 1)
                dve.tensor_tensor(x_t[u % 2], m_sq[:, 0:HALF], m_sq[:, HALF:], ALU.add).then_inc(amp2_done, 1)
                dve.wait_ge(amp_hi_done, u + 1)
                dve.tensor_tensor(act_lo[:, 3 * DC + mt, cols_of(half)], x_t[u % 2],
                                  act_hi[:, 3 * DC + mt, cols_of(half)].bitcast(F32),
                                  ALU.subtract).then_inc(amp_lo_done, 1)
            split(G_WO + 5, 0)
            split(G_WO + 6, 1)
            for half in range(2):
                M, S = mr_st[half][:, 0:HALF], mr_st[half][:, HALF:]
                dve.wait_ge(post_sums, half + 1)
                if half == 1:
                    split(G_WO + 7, 0, 2 * DC * P)
                dve.tensor_scalar(M, ps[half][:, 0:HALF], 1.0 / OUT, None, ALU.mult).then_inc(p_mean, 1)
                dve.wait_ge(p_mean, half + 1)
                dve.tensor_tensor(S, M, M, ALU.mult).then_inc(p_msq, 1)
                dve.wait_ge(p_msq, half + 1)
                dve.scalar_tensor_tensor(out=S, in0=ps[half][:, HALF:], scalar=1.0 / OUT, in1=S, op0=ALU.mult,
                                         op1=ALU.subtract).then_inc(p_var, 1)
                dve.wait_ge(p_var, half + 1)
                dve.tensor_scalar(S, S, 0.0, 1e-5, ALU.max, ALU.add).then_inc(p_eps, 1)
                dve.wait_ge(p_root, half + 1)
                dve.reciprocal(S, S).then_inc(p_inv, 1)
                dve.wait_ge(p_inv, half + 1)
                for mt in range(DC):
                    x = post[:, mt, cols_of(half)]
                    dve.tensor_tensor(x, x, M, ALU.subtract).then_inc(p_cent, 1)
                    dve.wait_ge(p_cent, half * DC + mt + 1)
                    dve.tensor_tensor(x, x, S, ALU.mult).then_inc(p_normed, 1)
                for mt in range(DC):
                    u = half * DC + mt
                    dve.wait_ge(z_hi_done, u + 1)
                    dve.tensor_tensor(act_lo[:, mt, cols_of(half)], post[:, mt, cols_of(half)],
                                      act_hi[:, mt, cols_of(half)].bitcast(F32), ALU.subtract).then_inc(z_lo_done, 1)
            for u in range(2 * DC + 1):
                if u < 2 * DC:
                    dve.wait_ge(top1_done, u + 1)
                    dve.wait_ge(top_in[u % 2], 16 * (u // 2 + 1))
                    if u == 0:
                        dve.wait_ge(post_sums, 2)
                    if u >= 2:
                        dve.wait_ge(h1_lo_done, u - 1)
                    dve.tensor_tensor(x_t[u % 2], acc_at(u % DC), top_x[u % 2], ALU.add).then_inc(x_done, 1)
                if u:
                    half, mt = (u - 1) // DC, (u - 1) % DC
                    dve.wait_ge(h1_hi_done, u)
                    dve.scalar_tensor_tensor(out=act_lo[:, DC + mt, cols_of(half)], in0=x_t[(u - 1) % 2], scalar=0.0,
                                             in1=act_hi[:, DC + mt, cols_of(half)].bitcast(F32), op0=ALU.max,
                                             op1=ALU.subtract).then_inc(h1_lo_done, 1)

        @block.gpsimd
        def _(pool):
            pool.memset(ident[:, :], 0.0).then_inc(ident_z, 1)
            pool.memset(zero[:, :], 0.0).then_inc(ident_z, 1)
            pool.memset(tiny[:, 0:1], 1e-37).then_inc(ident_z, 1)
            pool.memset(tiny[:, 1:2], 1e-8).then_inc(ident_z, 1)
            pool.memset(same_row[:, :], 1.0).then_inc(ident_z, 1)
            pool.wait_ge(ident_z, 5)
            pool.affine_select(out=ident[:, :], in_=ident[:, :], compare_op=ALU.not_equal, fill=1.0, base=0,
                               pattern=[[-1, P]], channel_multiplier=1).then_inc(masks, 1)
            pool.affine_select(out=same_row[:, :], in_=same_row[:, :], compare_op=ALU.is_ge, fill=0.0, base=0,
                               pattern=[[-N, P // N], [0, N]], channel_multiplier=1).then_inc(masks, 1)
            pool.wait_ge(masks, 2)
            pool.affine_select(out=same_row[:, :], in_=same_row[:, :], compare_op=ALU.is_ge, fill=0.0, base=N - 1,
                               pattern=[[N, P // N], [0, N]], channel_multiplier=-1).then_inc(masks, 1)
            pool.wait_ge(masks, 3)
            for qd in range(4):
                rows = slice(32 * qd, 32 * qd + 32)
                pool.tensor_copy(same_row32[rows, :], same_row[rows, rows]).then_inc(masks, 1)
            pool.wait_ge(masks, 7)
            pool.dma_start(ids_sb[:, :, :], ids.rearrange("(t p) n -> p t n", p=P)).then_inc(ids_in, 16)
            pool.wait_ge(ids_in, 16)
            for t in range(TILES_B):
                for i in range(N):
                    pool.indirect_dma_start(strength[:, t, N * i:N * (i + 1)], None, tbl[i],
                                            bass.IndirectOffsetOnAxis(ids_sb[:, t, i:i + 1], 0))\
                        .then_inc(strength_in, 16)
            pool.wait_ge(zeroed, 1)
            for stage in STAGES:
                name, g0, n = stage

                def step(j, p):
                    pool.wait_ge(evac, 2 * j + (p + 1))
                    pool.dma_start(OUTS[name][2 * j + (p - g0)], hout[p]).then_inc(stored[p], 16)
                    if name in ("l1_r", "l1_i"):
                        if is_block(j, p, KC):
                            pool.wait_ge(zeroed, 2)
                        if not is_block(j, p, 0):
                            pool.wait_ge(acc2_done, 2 * j + p)
                        pool.tensor_tensor(sq, hout[p], hout[p], ALU.mult).then_inc(sq_done, 1)
                        pool.wait_ge(sq_done, 2 * j + (p + 1))
                        pool.tensor_tensor(acc2, acc2, sq, ALU.add).then_inc(acc2_done, 1)
                    if is_block(j, p, KC):
                        pool.wait_ge(st_recip, 1)
                        pool.dma_start(stat_rows, st[0:1, :]).then_inc(st_saved, 16)

                blocks(pool, stage, step)
            for si, s in enumerate("ri"):
                def store(m, rows_of):
                    for mt in range(DC):
                        for half in range(2):
                            v = 2 * mt + half
                            pool.wait_ge(tile_evac, 2 * N * DC * m + (TILES_Q * si + N * (v + 1)))
                            pool.dma_start(rows_of(mt)[:, half * 2048:(half + 1) * 2048],
                                           misc[half]).then_inc(q_stored[half], 16)

                with pool.Fori(0, 2) as m:
                    store(m, lambda mt: qkT[s][mt // 2, m, mt % 2 * P:(mt % 2 + 1) * P])
                store(2, lambda mt: valT[s][mt * P:(mt + 1) * P])

            def step(t, g):
                if not (isinstance(t, int) and t == TILES_B):
                    for hh in range(2):
                        pool.wait_ge(ki_in[hh], 64 * t + 16 * (g + 1))
                        pool.tensor_tensor(qkk[hh][0:64, 2], zero[0:64, :, None].to_broadcast([64, HU, P]),
                                           qkk[hh][0:64, 2], ALU.subtract).then_inc(negated, 1)

            groups(pool, step)

            def add_squares(t, q):
                ns = slice(0, N) if q else slice(0, 1)
                pool.wait_ge(z_sq_done, 4 * t + (q + 1))
                pool.tensor_tensor(m2[q % 2][:, ns], z_sq[q % 2][:, 0, ns], z_sq[q % 2][:, 1, ns],
                                   ALU.add).then_inc(m2_done, 1)

            def split_negated(t, pos):
                pool.wait_ge(a_hi_done, 8 * t + 2 * (pos + 1))
                pool.tensor_tensor(w_lo[:, pos % 2, 1024:1536], w_hi[:, pos % 2, 512:1024].bitcast(F32),
                                   a_raw[:, 1].rearrange("p c x -> p (c x)"), ALU.subtract).then_inc(neg_lo_done, 1)

            for t, pos in [(0, 0), (0, 1), (0, 2), (0, 3), (1, 0)]:
                split_negated(t, pos)

            def step(t):
                pool.wait_ge(early_sq, t + 1)
                pool.tensor_tensor(m2[0][:, 1:N], z_sq[0][:, 0, 1:N], z_sq[0][:, 1, 1:N], ALU.add)\
                    .then_inc(early_m2, 1)
                add_squares(t, 0)
                for q in range(4):
                    Q1 = 4 * t + (q + 1)
                    pool.wait_ge(rinv_done, Q1)
                    pool.tensor_tensor(un[:, 1], z[:, q, 1], rt[q % 2], ALU.mult).then_inc(ui_done, 1)
                    pool.tensor_scalar(m2[q % 2], m2[q % 2], 0.0, None, ALU.is_equal).then_inc(zero_marked, 1)
                    if q in (1, 2):
                        add_squares(t, q + 1)
                    pool.wait_ge(ui_done, Q1)
                    if not (isinstance(t, int) and t == 0 and q == 0):
                        pool.wait_ge(t_done, Q1 - 1)
                    for d in range(1, N):
                        mm = pool.tensor_tensor(t_i[:, AT[d][0]:AT[d][1]], un[:, 1, 0:N - d], un[:, 1, d:N],
                                                ALU.mult)
                    if q:
                        mm.then_inc(t_mult, 1)
                        pool.wait_ge(zero_marked, Q1)
                        pool.wait_ge(t_mult, 3 * t + q)
                        for d in range(1, N):
                            part = t_i[:, AT[d][0]:AT[d][1]]
                            mm = pool.tensor_tensor(part, part, m2[q % 2][:, 0:N - d], ALU.add)
                    if q == 3:
                        mm.then_inc(ti_first, 1)
                        pool.wait_ge(ti_first, t + 1)
                        for d in range(1, N):
                            part = t_i[:, AT[d][0]:AT[d][1]]
                            mm = pool.tensor_tensor(part, part, m2[1][:, d:N], ALU.add)
                    mm.then_inc(ti_done, 1)
                    if q == 0:
                        add_squares(t, 1)
                    if q < 3 and not (isinstance(t, int) and t == TILES_B - 1):
                        split_negated(t + 1, q + 1)
                if not (isinstance(t, int) and t >= TILES_B - 2):
                    split_negated(t + 2, 0)

            tiles(pool, step)
            for k in range(2):
                pool.wait_ge(w_hi_done, G_WO + 3 + k)
                pool.tensor_tensor(w_lo[:, k, :], w_raw, w_hi[:, k, :].bitcast(F32),
                                   ALU.subtract).then_inc(w_lo_done, 1)

        @block.tensor
        def _(pe):
            def three(out, lhs_hi, lhs_lo, rhs_hi, rhs_lo, start, stop):
                pe.matmul(out, lhs_hi, rhs_hi, start=start, stop=False)
                pe.matmul(out, lhs_hi, rhs_lo, start=False, stop=False)
                return pe.matmul(out, lhs_lo, rhs_hi, start=False, stop=stop)

            def wide(j, p, k=None):
                pe.wait_ge(w_lo_done, 2 * j + (p + 1))
                if not (isinstance(j, int) and j == 0):
                    pe.wait_ge(evac, 2 * j + p - 1)
                for c in range(KC):
                    if k is not None:
                        pe.wait_ge(act_lo_done, KC * k + c + 1)
                    for half in range(2):
                        cs = slice(half * HALF, (half + 1) * HALF)
                        mm = three(ps[p][:, cs], w_hi[:, p, c * P:(c + 1) * P], w_lo[:, p, c * P:(c + 1) * P],
                                   act_hi[:, c, cs], act_lo[:, c, cs], c == 0, c == KC - 1)
                    mm.then_inc(used, 1)

            def sums(s):
                pe.wait_ge(acc_done, KC * (s + 1))
                pe.wait_ge(acc2_done, KC * (s + 1))
                pe.wait_ge(ones_done, 1)
                if s == 1:
                    pe.wait_ge(st_var, 1)
                for half in range(2):
                    cs = slice(half * HALF, (half + 1) * HALF)
                    pe.matmul(ps_st[0][:, cs], ones[:, :], acc[:, cs], start=True, stop=True)
                    mm = pe.matmul(ps_st[1][:, cs], ones[:, :], acc2[:, cs], start=True, stop=True)
                mm.then_inc(sums_done, 1)

            FIRST = {"l1_r": 0, "l2_r": 1, "l2_i": 2}
            for stage in STAGES:
                name, g0, n = stage

                def step(j, p):
                    wide(j, p, FIRST[name] if name in FIRST and is_block(j, p, g0) else None)
                    if is_block(j, p, KC) or is_block(j, p, G_TOP):
                        sums(int(g0 == G_TOP))

                blocks(pe, stage, step)

            for si, s in enumerate("ri"):
                T0 = TILES_Q * si

                def matrix(m, first):
                    for e in range(2):
                        pe.wait_ge(w_lo_done, 2 * m + (G_END + 6 * si + e + 1))
                        for mt in range(2 * e, 2 * e + 2):
                            for half in range(2):
                                cs = slice(half * HALF, (half + 1) * HALF)
                                for n in range(N):
                                    i = (mt * 2 + half) * N + n
                                    if not (first and si == 0 and i < 4):
                                        pe.wait_ge(tile_evac, 2 * N * DC * m + (T0 + i - 3))
                                    for kc in range(DC):
                                        c = n * DC + kc
                                        if first and mt == 0 and half == 0:
                                            pe.wait_ge(act_lo_done, KC * (3 + si) + c + 1)
                                        ws = slice((mt % 2 * DC + kc) * P, (mt % 2 * DC + kc + 1) * P)
                                        mm = three(ps_st[i // 2 % 2][:, (i % 2) * HALF:(i % 2 + 1) * HALF],
                                                   w_hi[:, e, ws], w_lo[:, e, ws],
                                                   act_hi[:, c, cs], act_lo[:, c, cs], kc == 0, kc == DC - 1)
                                    mm.then_inc(tile_done, 1)

                matrix(0, True)
                with pe.Fori(1, 3) as m:
                    matrix(m, False)

            pe.wait_ge(evac, G_END)
            pe.wait_ge(tile_evac, 2 * TILES_Q)
            pe.wait_ge(masks, 1)

            def step(t, g):
                start, end = isinstance(t, int) and t == 0, isinstance(t, int) and t == TILES_B
                k1 = 4 * t + (g - 1)

                def scores(hh):
                    U1 = 8 * t + (2 * g + hh + 1)
                    pe.wait_ge(negated, U1)
                    pe.wait_ge(qk_in[hh], 192 * t + 48 * (g + 1))
                    if not (start and g == 0):
                        pe.wait_ge(diag_done, 32 * t + (8 * g + 4 * hh - 4))
                    for h in range(HU):
                        mm = pe.matmul(ps[hh][:, h * 256:(h + 1) * 256], qkk[hh][:, 0, h],
                                       qkk[hh][:, 1:3, h], start=True, stop=True)
                    mm.then_inc(scores_done, 1)

                if not (start and g < 2):
                    pe.wait_ge(v_in, 32 * k1)
                    if not (start and g == 2):
                        for e in range(2):
                            pe.wait_ge(wT_done[e], k1 - 1)
                    if not start:
                        pe.wait_ge(a_out_done, 8 * t if g > 1 else 8 * t - 8)
                    for si in range(2):
                        for c in range(DC):
                            mm = pe.transpose(ps_st[0][:, si * 512 + c * P:si * 512 + (c + 1) * P],
                                              v_raw[:, si, c, :], ident[:, :])
                        mm.then_inc(vT_done, 1)
                if not end:
                    scores(0)
                if not (start and g < 2):
                    for e in range(2):
                        pe.wait_ge(z_done, 2 * k1 + (e - 1))
                        pe.wait_ge(v_nat_done, 2 * k1 + (e - 1))
                        for h in range(4):
                            mm = pe.transpose(ps_st[0][:, e * 512 + h * P:e * 512 + (h + 1) * P],
                                              z_w[g % 2][:, 4 * e + h, :], ident[:, :])
                        mm.then_inc(zT_done, 1)
                if not end:
                    scores(1)
                if not (start and g < 2):
                    if not (start and g == 2):
                        pe.wait_ge(o_lo_done, 2 * k1 - 2)
                    for si in range(2):
                        for h in range(H):
                            if si == 0 and h % 4 == 0:
                                pe.wait_ge(wT_done[h // 4], k1)
                            lo = 64 * (h % 2)
                            mm = pe.matmul(ps_st[1][lo:lo + 64, si * 512 + h // 2 * P:si * 512 + (h // 2 + 1) * P],
                                           v_nat[:, si, h * HD:(h + 1) * HD], wT[:, h, :], start=True, stop=True)
                        mm.then_inc(pv_done, 1)
                if g == 1 and not start:
                    pe.wait_ge(w_lo_done, G_WO + 2)
                    pe.wait_ge(o_lo_done, 8 * t)
                    for i in range(2 * DC):
                        si, mt = i // DC, i % DC
                        if i >= 2:
                            pe.wait_ge(a_out_done, 8 * t + (i - 9))
                        for kc in range(DC):
                            ws = slice((mt * DC + kc) * P, (mt * DC + kc + 1) * P)
                            mm = three(ps_st[0][:, (i % 2) * 512:(i % 2 + 1) * 512], w_hi[:, si, ws], w_lo[:, si, ws],
                                       act_hi[:, kc, si * HALF:(si + 1) * HALF],
                                       act_lo[:, kc, si * HALF:(si + 1) * HALF],
                                       kc == 0, kc == DC - 1)
                        mm.then_inc(wo_done, 1)

            groups(pe, step)

            acc_of = [ps[0], ps[1], ps_st[0], ps_st[1]]
            pe.wait_ge(diag_done, 4 * 2 * GROUPS)
            pe.wait_ge(a_out_done, 2 * DC * TILES_B)
            pe.wait_ge(o_lo_done, 2 * GROUPS)

            def interact(t, turn=False):
                start = isinstance(t, int) and t == 0
                for pos in range(N):
                    n, e = (pos + 1) % N, pos % 2
                    if start and pos in (0, N - 1):
                        pe.wait_ge(wi_lo_done, 16 if pos else 12)
                    if not start:
                        pe.wait_ge(z_out, 8 * t + (pos - 3))
                    if pos == 1 and turn:
                        turn_sup(t - 1)
                    if pos == N - 1 and turn:
                        pe.wait_ge(supT_out, 2 * t - 2)
                    pe.wait_ge(a_lo_done, 4 * t + (pos + 1))
                    pe.wait_ge(neg_lo_done, 4 * t + (pos + 1))
                    for im in range(2):
                        out = acc_of[pos][:, im * 512:(im + 1) * 512]
                        for kc in range(DC):
                            for si in range(2):
                                a0 = (si if im else 2 * si) * 512 + kc * P
                                wc, wo = DC * n + 2 * (si ^ im) + kc // 2, (kc % 2) * 512
                                mm = three(out, w_hi[:, e, a0:a0 + P], w_lo[:, e, a0:a0 + P],
                                           act_hi[:, wc, wo:wo + 512], act_lo[:, wc, wo:wo + 512],
                                           kc == 0 and si == 0, kc == DC - 1 and si == 1)
                    mm.then_inc(int_done, 1)

            def turn_sup(t1):
                pe.wait_ge(scaled, t1)
                if isinstance(t1, int) and t1 == TILES_B:
                    pe.wait_ge(supT_out, 2 * t1 - 2)
                else:
                    pe.wait_ge(z_out, 8 * t1 + 8)
                for e in range(2):
                    for c in range(DC):
                        mm = pe.transpose(ps_st[1][:, e * 512 + c * P:e * 512 + (c + 1) * P],
                                          sup[:, e, c * P:(c + 1) * P], ident[:, :])
                    mm.then_inc(supT_done, 1)

            interact(0)

            def step(t):
                if not (isinstance(t, int) and t == TILES_B - 1):
                    interact(t + 1, not (isinstance(t, int) and t == 0))
                else:
                    turn_sup(t)

            tiles(pe, step)
            turn_sup(TILES_B)

            pe.wait_ge(w_lo_done, G_WO + 4)
            for u in range(2 * DC):
                half, mt = u // DC, u % DC
                cs = cols_of(half)
                if mt == 0:
                    pe.wait_ge(m_lo_done, DC * (half + 1))
                if u >= 2:
                    pe.wait_ge(m_sq_done, u - 1)
                for im in range(2):
                    for si in range(2):
                        for kc in range(DC):
                            ws = slice((mt * DC + kc) * P, (mt * DC + kc + 1) * P)
                            c = (si if im else 2 * si) * DC + kc
                            e = si ^ im
                            mm = three(ps[u % 2][:, im * 512:(im + 1) * 512], w_hi[:, e, ws], w_lo[:, e, ws],
                                       act_hi[:, c, cs], act_lo[:, c, cs],
                                       kc == 0 and si == 0, kc == DC - 1 and si == 1)
                mm.then_inc(meas_done, 1)

            def layer(out, e, mt, half, c0):
                for kc in range(DC):
                    ws = slice((mt * DC + kc) * P, (mt * DC + kc + 1) * P)
                    mm = three(out, w_hi[:, e, ws], w_lo[:, e, ws], act_hi[:, c0 + kc, cols_of(half)],
                               act_lo[:, c0 + kc, cols_of(half)], kc == 0, kc == DC - 1)
                return mm

            pe.wait_ge(w_lo_done, G_WO + 5)
            pe.wait_ge(supT_out, 2 * TILES_B)
            for half in range(2):
                pe.wait_ge(amp_lo_done, DC * (half + 1))
                for mt in range(DC):
                    if half:
                        pe.wait_ge(post_out, mt + 1)
                    layer(acc_at(mt), 0, mt, half, 3 * DC).then_inc(post_done, 1)
                pe.wait_ge(m_sq_done, 2 * DC)
                for mt in range(DC):
                    pe.wait_ge(post_out, DC * half + mt + 1)
                    pe.matmul(ps[half][:, 0:HALF], ones[:, :], post[:, mt, cols_of(half)],
                              start=(mt == 0), stop=(mt == DC - 1))
                for mt in range(DC):
                    pe.wait_ge(post_sq_done, DC * half + mt + 1)
                    mm = pe.matmul(ps[half][:, HALF:], ones[:, :], post_sq[:, mt],
                                   start=(mt == 0), stop=(mt == DC - 1))
                mm.then_inc(post_sums, 1)
            pe.wait_ge(w_lo_done, G_WO + 6)
            for half in range(2):
                pe.wait_ge(z_lo_done, DC * (half + 1))
                for mt in range(DC):
                    if half:
                        pe.wait_ge(x_done, mt + 1)
                    else:
                        pe.wait_ge(post_out, 2 * DC)
                    layer(acc_at(mt), 1, mt, half, 0).then_inc(top1_done, 1)
            pe.wait_ge(w_lo_done, G_WO + 7)
            for half in range(2):
                pe.wait_ge(h1_lo_done, DC * (half + 1))
                for mt in range(2):
                    layer(ps[half][:, mt * 512:(mt + 1) * 512], 0, mt, half, DC).then_inc(top2_done, 1)
            pe.wait_ge(x_done, 2 * DC)
            for half in range(2):
                pe.wait_ge(h2_done, 2 * half + 2)
                for kc in range(2):
                    c0 = COLS["w_top3"] + kc
                    mm = pe.matmul(acc_at(half)[0:1, :], par[:, c0:c0 + 1], post[:, kc, cols_of(half)],
                                   start=(kc == 0), stop=(kc == 1))
                mm.then_inc(y_done, 1)


def block_layout(WT):
    K, M = WT.shape
    return WT.reshape(K // P, P, M // P, P).transpose(2, 1, 0, 3).reshape(M // P, P, K)


def kernel(**inputs):
    import numpy as np
    import concourse.bacc as bacc
    from concourse.bass_utils import run_bass_kernel_spmd

    a = {k: np.asarray(v) for k, v in inputs.items()}
    L = {k[7:]: v for k, v in a.items() if k.startswith("L0_rec_")}
    host = {"xT": a["r_x"].T.reshape(KC, P, B), "ids": a["ids"]}
    for i in range(4):
        host[f"tbl_{i}"] = a[f"tbl_{i}"]
    W = {"l1_r": block_layout(L["er_W1"].T), "l1_i": block_layout(L["ei_W1"].T),
         "l2_r": block_layout(L["er_W2"].T), "l2_i": block_layout(L["ei_W2"].T),
         "top1x": block_layout(a["W_top1"][OUT:])}
    for s in "ri":
        W["qkv_" + s] = np.stack([block_layout(L[f"W{m}_{s}"].T).transpose(1, 0, 2).reshape(P, BLK)
                                  for m in "qkv"])
    W["o"] = np.stack([block_layout(L["Wo_" + s].T).transpose(1, 0, 2).reshape(P, BLK) for s in "ri"])
    pieces = np.stack([L["int_Wr"], L["int_Wi"]], axis=1).transpose(0, 1, 3, 2)
    pieces = pieces.reshape(N, 2, 2, 2, P, D).transpose(0, 1, 2, 4, 3, 5).reshape(N, 4, P, 2 * D)
    W["int"] = pieces[[1, 2, 3, 0]].reshape(4 * N, P, 2 * D)
    W["meas"] = np.stack([block_layout(L["meas_M" + s].T).transpose(1, 0, 2).reshape(P, BLK) for s in "ri"])
    W["post"] = block_layout(L["post_W"].T).transpose(1, 0, 2).reshape(P, BLK)
    W["top1z"] = block_layout(a["W_top1"][:OUT]).transpose(1, 0, 2).reshape(P, BLK)
    W["top2"] = block_layout(a["W_top2"]).transpose(1, 0, 2).reshape(P, 2 * DC * P)
    for k, v in W.items():
        host["w_" + k] = v

    def col(v):
        return v.reshape(-1, P).T

    parts = {"b1_r": L["er_b1"], "b1_i": L["ei_b1"], "b_top1": a["b_top1"], "b2_r": L["er_b2"],
             "b2_i": L["ei_b2"], "g_r": L["er_g1"], "be_r": L["er_be1"], "g_i": L["ei_g1"], "be_i": L["ei_be1"],
             "bqkv_r": np.concatenate([L["bq_r"], L["bk_r"], L["bv_r"]]),
             "bqkv_i": np.concatenate([L["bq_i"], L["bk_i"], L["bv_i"]]),
             "bo_r": L["bo_r"], "bo_i": L["bo_i"], "post_b": L["post_b"], "post_g": L["post_g"],
             "post_be": L["post_be"], "b_top2": a["b_top2"], "w_top3": a["W_top3"]}
    host["cols"] = np.concatenate([col(parts[k]) for k in COLS], axis=1)
    host = {k: np.ascontiguousarray(v) for k, v in host.items()}

    nc = bacc.Bacc("TRN2", target_bir_lowering=False, num_devices=1)
    t = {k: nc.dram_tensor("in_" + k, list(v.shape), mybir.dt.from_np(v.dtype), kind="ExternalInput").ap()
         for k, v in host.items()}
    y = nc.dram_tensor("y", [1, B], F32, kind="ExternalOutput").ap()
    build(nc, t["xT"], t["ids"], [t[f"tbl_{i}"] for i in range(4)],
          {k[2:]: v for k, v in t.items() if k[:2] == "w_"}, t["cols"], y)
    r = run_bass_kernel_spmd(nc, [{"in_" + k: v for k, v in host.items()}], core_ids=[0])
    return np.asarray(r.results[0]["y"]).reshape(B, 1)
```
